# Optimizing a Trainium2 kernel written in Bass

```python
import numpy as np
import jax
import jax.numpy as jnp

def _softmax(x, axis=-1):
    return jax.nn.softmax(x, axis=axis)
def _gelu(x):
    return jax.nn.gelu(x, approximate=True)
def _silu(x):
    return jax.nn.silu(x)
def _sigmoid(x):
    return jax.nn.sigmoid(x)
def _layernorm(x, axis=-1, eps=1e-5):
    m = jnp.mean(x, axis=axis, keepdims=True)
    v = jnp.var(x, axis=axis, keepdims=True)
    return (x - m) / jnp.sqrt(v + eps)
def _scatter_add(tgt, idx, src, axis=0):
    return tgt.at[idx].add(src)
def _segment_sum(src, seg, n):
    return jax.ops.segment_sum(src, seg, n)

kernel_name = 'mk_adj_resnorm_d2_adj_128_3da25b'

def setup_inputs(seed: int = 0):
    np.random.seed(seed)
    _w = jnp.asarray
    def _rec_inputs():
        import jax
        import jax.numpy as jnp
        _gk = jax.random.key(seed)
        x = -0.0005207 + 1.001 * jax.random.normal(jax.random.fold_in(_gk, 1), (4096, 128), jnp.float32)
        _a = jax.random.bernoulli(jax.random.fold_in(_gk, 2), 0.00195312, (4096, 4096))
        _a = jnp.logical_or(_a, jnp.swapaxes(_a, -1, -2))
        _a = jnp.logical_or(_a, jnp.eye(4096, dtype=bool))
        _af = _a.astype(jnp.float32)
        _af = _af * jax.random.uniform(jax.random.fold_in(_gk, 3), (4096, 4096), jnp.float32, 0.05, 1)
        adj = _af
        return x, adj
    x, adj = _rec_inputs()
    def _L0_gnn_setup():
        import jax, jax.numpy as jnp
        import numpy as np
        key = jax.random.key(seed)
        k1, k2, k3, k4 = jax.random.split(key, 4)
        n, in_dim, out_dim = (16384, 128, 128)
        h = jax.random.normal(k1, (n, in_dim), dtype=jnp.float32)
        adj = jax.random.uniform(k2, (n, n), dtype=jnp.float32)
        W_self = jax.random.normal(k3, (in_dim, out_dim), dtype=jnp.float32) * (1.0 / np.sqrt(in_dim))
        W_neigh = jax.random.normal(k4, (in_dim, out_dim), dtype=jnp.float32) * (1.0 / np.sqrt(in_dim))
        return {'h': h, 'adj': adj, 'W_self': W_self, 'W_neigh': W_neigh}
    _L0_gnn_all = _L0_gnn_setup()
    _L0_gnn_in = {k: v for k, v in _L0_gnn_all.items() if k in ('W_self', 'W_neigh', )}
    del _L0_gnn_all

    def _L1_gnn_setup():
        import jax, jax.numpy as jnp
        import numpy as np
        N = 1024
        IN_DIM = 128
        OUT_DIM = 128
        HEADS = 4

        def _gatv2_head(x, A_shape, w1, w2, a, Wlin):
            x1 = x @ w1
            x2 = x @ w2
            E = jax.nn.leaky_relu(x1[:, None, :] + x2[None, :, :], negative_slope=0.01)
            s = E @ a
            s = jnp.tanh(s / 8.0) * 8.0
            s = jnp.exp(s) * A_shape
            s = s / jnp.sum(s, axis=-1, keepdims=True)
            out = s @ x @ Wlin.T
            return jax.nn.leaky_relu(out, negative_slope=0.01)
        key = jax.random.key(seed)
        ks = jax.random.split(key, 7)
        x = jax.random.normal(ks[0], (N, IN_DIM), dtype=jnp.float32)
        A_shape = jax.random.uniform(ks[1], (N, N), dtype=jnp.float32)
        w1 = jax.random.normal(ks[2], (HEADS, IN_DIM, OUT_DIM), dtype=jnp.float32)
        w2 = jax.random.normal(ks[3], (HEADS, IN_DIM, OUT_DIM), dtype=jnp.float32)
        a = jax.random.normal(ks[4], (HEADS, OUT_DIM), dtype=jnp.float32)
        Wlin = jax.random.normal(ks[5], (HEADS, OUT_DIM, IN_DIM), dtype=jnp.float32) * (1.0 / np.sqrt(IN_DIM))
        w = jax.random.normal(ks[6], (OUT_DIM * HEADS, OUT_DIM), dtype=jnp.float32)
        return {'x': x, 'A_shape': A_shape, 'w1': w1, 'w2': w2, 'a': a, 'Wlin': Wlin, 'w': w}
    _L1_gnn_all = _L1_gnn_setup()
    _L1_gnn_in = {k: v for k, v in _L1_gnn_all.items() if k in ('w1', 'w2', 'a', 'Wlin', 'w', )}
    del _L1_gnn_all

    return {
        "x": x,
        "adj": adj,
        "L0_gnn_W_self": _L0_gnn_in["W_self"],
        "L0_gnn_W_neigh": _L0_gnn_in["W_neigh"],
        "L1_gnn_w1": _L1_gnn_in["w1"],
        "L1_gnn_w2": _L1_gnn_in["w2"],
        "L1_gnn_a": _L1_gnn_in["a"],
        "L1_gnn_Wlin": _L1_gnn_in["Wlin"],
        "L1_gnn_w": _L1_gnn_in["w"],
    }

def reference(x, adj, L0_gnn_W_self, L0_gnn_W_neigh, L1_gnn_w1, L1_gnn_w2, L1_gnn_a, L1_gnn_Wlin, L1_gnn_w):
    import jax
    import jax.numpy as jnp
    def _L0_gnn_ref(h, adj, W_self, W_neigh):
        import jax, jax.numpy as jnp
        import numpy as np
        deg = jnp.clip(jnp.sum(adj, axis=1, keepdims=True), 1.0)
        h_neigh = adj @ h / deg
        return h @ W_self + h_neigh @ W_neigh

    def _L1_gnn_ref(x, A_shape, w1, w2, a, Wlin, w):
        import jax, jax.numpy as jnp
        import numpy as np
        N = 1024
        IN_DIM = 128
        OUT_DIM = 128
        HEADS = 4

        def _gatv2_head(x, A_shape, w1, w2, a, Wlin):
            x1 = x @ w1
            x2 = x @ w2
            E = jax.nn.leaky_relu(x1[:, None, :] + x2[None, :, :], negative_slope=0.01)
            s = E @ a
            s = jnp.tanh(s / 8.0) * 8.0
            s = jnp.exp(s) * A_shape
            s = s / jnp.sum(s, axis=-1, keepdims=True)
            out = s @ x @ Wlin.T
            return jax.nn.leaky_relu(out, negative_slope=0.01)
        heads = [_gatv2_head(x, A_shape, w1[h], w2[h], a[h], Wlin[h]) for h in range(w1.shape[0])]
        return jnp.concatenate(heads, axis=-1) @ w

    x = _layernorm(x + _L0_gnn_ref(x, adj, L0_gnn_W_self, L0_gnn_W_neigh), axis=-1)
    x = _layernorm(x + _L1_gnn_ref(x, adj, L1_gnn_w1, L1_gnn_w2, L1_gnn_a, L1_gnn_Wlin, L1_gnn_w), axis=-1)
    return x


_drawn_inputs = setup_inputs


def setup_inputs(seed=0):
    import zlib

    import numpy as np

    out = dict(_drawn_inputs(seed))
    spreads = {}
    factors = {}
    for name, (base, spread) in spreads.items():
        noise = np.random.default_rng([zlib.crc32(name.encode()), seed]).standard_normal(out[name].shape)
        drawn = base * np.exp(spread * noise) if base else spread * noise
        out[name] = jnp.asarray(drawn.astype(out[name].dtype))
    for name, factor in factors.items():
        out[name] = (out[name] * factor).astype(out[name].dtype)
    return out
```

```python
import concourse.bass as bass
from concourse import mybir
from contextlib import ExitStack


def two_layer_graph_kernel(nc, x, x_t, adj, adj_t, w_self, w_neigh, w1, w2, w1_t, w2_t, a_row, a_col,
                           wlin_t, w_out, lane, columns, out):
    F32, I32, U32 = mybir.dt.float32, mybir.dt.int32, mybir.dt.uint32
    BF16 = mybir.dt.bfloat16
    ALU = mybir.AluOpType
    ACT = mybir.ActivationFunctionType
    AX = mybir.AxisListType.X

    P = 128
    N, D = x.shape
    H = w1.shape[0]
    HD = H * D
    T = N // P
    TS = 4
    STRIPS = T // TS
    SW = TS * P
    PIECES = 4
    JT = T // PIECES
    CH = 256
    NCH = N // CH
    CAND = 8 * NCH
    ROUNDS = 5
    SLOTS = 8 * ROUNDS
    BLOCK = 64
    NBLK = N // BLOCK
    G = 4
    HALVES = 2
    TURNS = BLOCK // G // HALVES
    KEY = 17
    ROWJ = HD + H + D + 1
    ROWI = HD + H
    ZW = HD + H
    XW = D + 1
    EPS = 1e-5
    SLOPE = 0.01
    LOADS = 12
    LIN = SLOPE
    POS = 1 - SLOPE

    table_j = nc.dram_tensor("table_j", [N, ROWJ], F32, kind="Internal").ap()
    table_i = nc.dram_tensor("table_i", [N, ROWI], F32, kind="Internal").ap()

    ctx = ExitStack()
    with ctx:
        def sb(name, shape, dt=F32):
            return ctx.enter_context(nc.sbuf_tensor(name, shape, dt))

        def ps(name, shape):
            return ctx.enter_context(nc.psum_tensor(name, shape, F32))

        def sem(name):
            return ctx.enter_context(nc.semaphore(name))

        ident = sb("ident", [P, P])
        xp_all = sb("xp_all", [P, T, D])
        slot_idx = sb("slot_idx", [P, T * BLOCK], I32)
        slot_val = sb("slot_val", [P, T * BLOCK])
        ctl = sb("ctl", [1, 4 * T + 2], I32)
        a_bc = sb("a_bc", [P, HD])
        wlin_sb = sb("wlin_sb", [P, H, D])
        wout_sb = sb("wout_sb", [P, H, D])
        wself_sb = sb("wself_sb", [P, D])
        wneigh_sb = sb("wneigh_sb", [P, D])
        w1_sb = sb("w1_sb", [P, H, D])
        w2_sb = sb("w2_sb", [P, H, D])
        v1_sb = sb("v1_sb", [P, H])
        v2_sb = sb("v2_sb", [P, H])
        big = sb("big", [P, PIECES * JT * SW])
        adjT_sb = big[:, :].rearrange("p (q j i) -> p q j i", q=PIECES, j=JT)
        agg_all = big[:, :].rearrange("p (t c) -> p t c", t=T)
        z_all = sb("z_all", [P, T, H])
        AREA = 24 * 1024
        area = sb("area", [P, AREA])
        used = [0]

        def cut(n, dt=F32):
            at = used[0]
            used[0] += n
            assert used[0] <= AREA, used[0]
            v = area[:, at:at + n]
            return v if dt is F32 else v.bitcast(dt)

        nat = [cut(N) for _ in range(2)]
        junk = cut(N // 2, BF16)
        h_sb = cut(T * D).rearrange("p (t d) -> p t d", t=T)
        xTs = cut(SW)
        aggT = cut(SW)
        xpT = cut(SW)
        cand = [cut(CAND) for _ in range(2)]
        cand_i = [cut(CAND, U32) for _ in range(2)]
        keep = cut(CAND)
        comp = [[cut(CAND) for _ in range(3)] for _ in range(2)]
        part = [cut(CAND, I32) for _ in range(3)]
        best = cut(3 * TS * SLOTS).rearrange("p (c k s) -> p c k s", c=3, k=TS)
        dec = cut(3 * TS * SLOTS, I32).rearrange("p (c k s) -> p c k s", c=3, k=TS)
        dec_i = cut(TS * SLOTS, I32).rearrange("p (k s) -> p k s", k=TS)
        lane_sb = cut(CAND)
        row_j = [cut(ROWJ) for _ in range(2)]
        row_i = [cut(ROWI) for _ in range(2)]
        yA = cut(SW)
        xpA = cut(SW)
        stat = cut(TS * 6).rearrange("p (k c) -> p k c", k=TS)
        mv = cut(TS * 2).rearrange("p (k c) -> p k c", k=TS)
        rstd = cut(TS)
        rdeg = cut(TS)
        deg_all = cut(T)
        cnt_all = cut(T)
        neg_all = cut(T)
        found = cut(T)
        both = cut(2 * T)
        acol_sb = cut(H)
        w12t = cut(2 * HD).rearrange("p (w h c) -> p w h c", w=2, h=H)
        peak = cut(1)
        crow = cut(8 * T)
        irow = cut(4 * T, I32)
        layer0_end = used[0]

        used[0] = 0
        g_sb = [cut(G * ROWJ).rearrange("p (r c) -> p r c", r=G) for _ in range(HALVES)]
        z_sb = [cut(G * ZW).rearrange("p (r c) -> p r c", r=G) for _ in range(HALVES)]
        sc_sb = [cut(G * H) for _ in range(HALVES)]
        th_sb = [cut(G * H) for _ in range(HALVES)]
        e_sb = [cut(G * H) for _ in range(HALVES)]
        xv_sb = [cut(G * XW).rearrange("p (r c) -> p r c", r=G) for _ in range(HALVES)]
        sx_sb = [cut(G * H * XW).rearrange("p (r h c) -> p r h c", r=G, h=H) for _ in range(HALVES)]
        idx_sb = [cut(G, I32) for _ in range(HALVES)]
        xi_sb = [cut(ROWI) for _ in range(2)]
        zeros = cut(HD)
        used[0] = 0
        aggn = cut(TS * HD).rearrange("p (k c) -> p k c", k=TS)
        aggnT = cut(H * SW).rearrange("p (h i) -> p h i", h=H)
        ylin = cut(H * SW).rearrange("p (h i) -> p h i", h=H)
        yleak = cut(H * SW).rearrange("p (h i) -> p h i", h=H)
        yC = cut(SW)
        oC = cut(SW)
        statC = cut(TS * 6).rearrange("p (k c) -> p k c", k=TS)
        mvC = cut(TS * 2).rearrange("p (k c) -> p k c", k=TS)
        rstdC = cut(TS)
        rzC = cut(TS * H)
        eps = sb("eps", [P, 1])

        banks = [ps(f"bank{i}", [P, 512]) for i in range(8)]
        b_aggT, b_n, b_s, b_x, b_1, b_2, b_pq, b_ctl = banks
        agg_ps = [banks[0], banks[1]]
        z_ps = [banks[2], banks[3]]
        lin_ps = banks[0:4]
        bT_ps = banks[4:6]
        bO_ps = banks[6]

        s_w = sem("weights_in")
        s_xT = sem("xT_in")
        s_nat = [sem(f"nat_in{b}") for b in range(2)]
        s_adjT = [sem(f"adjT_in{q}") for q in range(PIECES)]
        s_ident = sem("ident_ready")
        s_const = sem("dve_consts")
        s_abc = sem("a_bc_ready")
        s_v = sem("v_products")
        s_vsb = sem("v_ready")
        s_natdve = sem("nat_searched")
        s_natact = sem("nat_counted")
        s_pass = sem("nat_passes")
        s_piece = sem("adjT_used")
        s_aggT = sem("aggT_copied")
        s_ns = sem("layer0_products")
        s_var = sem("var_ready")
        s_std = sem("std_ready")
        s_xp = sem("xp_ready")
        s_xpTps = sem("xpT_transposed")
        s_xpT = sem("xpT_copied")
        s_pq = sem("pq_products")
        s_12 = sem("x12_products")
        s_12c = sem("x12_copied")
        s_xpall = sem("xp_kept")
        s_rx = sem("row_xp_copied")
        s_rows = [sem(f"rows_stored{b}") for b in range(2)]
        s_chain = sem("dve_chain")
        s_bothT = sem("stats_transposed")
        s_peak = sem("peak_ready")
        s_peakT = sem("peak_row")
        s_ctl = sem("ctl_ready")
        s_xi = [sem(f"xi_in{b}") for b in range(2)]
        s_blk = sem("block_in")
        s_pdve = sem("dve_waits_passed")
        s_ppool = sem("pool_waits_passed")
        s_psp = sem("sp_waits_passed")
        s_zero = sem("zeros_ready")
        s_idx = [sem(f"idx_copied{b}") for b in range(HALVES)]
        s_g = [sem(f"gathered{b}") for b in range(HALVES)]
        s_z = [sem(f"z_ready{b}") for b in range(HALVES)]
        s_acc = [sem(f"sums_ready{b}") for b in range(HALVES)]
        s_sc = [sem(f"scores_ready{b}") for b in range(HALVES)]
        s_th = [sem(f"tanh_ready{b}") for b in range(HALVES)]
        s_e = [sem(f"exp_ready{b}") for b in range(HALVES)]
        s_xv = [sem(f"xv_ready{b}") for b in range(HALVES)]
        s_sx = [sem(f"sx_ready{b}") for b in range(HALVES)]
        s_sum = [sem(f"sx_summed{b}") for b in range(HALVES)]
        s_tdve = sem("tile_scored")
        s_tpe = sem("tile_summed")
        s_evac = sem("tile_copied")
        s_rz = sem("rz_ready")
        s_aggn = sem("aggn_ready")
        s_aTps = sem("aggnT_transposed")
        s_aT = sem("aggnT_copied")
        s_lin = sem("lin_products")
        s_linc = sem("lin_copied")
        s_leak = sem("leaky_ready")
        s_o = sem("out_products")
        s_cC = sem("dve_chain_last")
        s_varC = sem("varC_ready")
        s_stdC = sem("stdC_ready")
        s_oC = sem("out_ready")
        s_out = sem("out_stored")

        CTL_A, CTL_B, CTL_A0, CTL_B0, CTL_NB, CTL_GEN = 0, T, 2 * T, 3 * T, 4 * T, 4 * T + 1

        def ctl_value(eng, at, low, high):
            return eng.value_load(ctl[0:1, bass.ds(at, 1)], min_val=low, max_val=high)

        MAXN = T * NBLK * TURNS

        def tile_counts(eng, t):
            return (ctl_value(eng, t + CTL_A, 1, TURNS), ctl_value(eng, t + CTL_B, 0, TURNS),
                    ctl_value(eng, t + CTL_A0, 0, MAXN), ctl_value(eng, t + CTL_B0, 0, MAXN))

        def apart(eng, passed):
            eng.sem_inc(passed, 1)

        block = ctx.enter_context(nc.Block())

        @block.sync
        def _(sp):
            sp.dma_start(h_sb, x.rearrange("(t p) d -> p t d", p=P)).then_inc(s_w, 16)
            sp.dma_start(lane_sb, lane.to_broadcast((P, CAND))).then_inc(s_w, 16)
            sp.dma_start(wself_sb[:, :], w_self).then_inc(s_w, 16)
            sp.dma_start(wneigh_sb[:, :], w_neigh).then_inc(s_w, 16)
            sp.dma_start(w1_sb[:, :, :], w1.rearrange("h c k -> c h k")).then_inc(s_w, 16)
            sp.dma_start(w2_sb[:, :, :], w2.rearrange("h c k -> c h k")).then_inc(s_w, 16)
            sp.dma_start(w12t[:, 0], w1_t.rearrange("h k c -> k h c")).then_inc(s_w, 16)
            sp.dma_start(w12t[:, 1], w2_t.rearrange("h k c -> k h c")).then_inc(s_w, 16)
            sp.dma_start(acol_sb, a_col).then_inc(s_w, 16)
            sp.dma_start(a_bc[:, :], a_row.to_broadcast((P, HD))).then_inc(s_w, 16)
            sp.dma_start(wlin_sb[:, :, :], wlin_t.rearrange("h d o -> d h o")).then_inc(s_w, 16)
            sp.dma_start(wout_sb[:, :, :], w_out.rearrange("(h o) n -> o h n", h=H)).then_inc(s_w, 16)
            with sp.Fori(0, STRIPS) as s:
                for k in range(TS):
                    sp.wait_ge(s_natdve, s * TS + (k + 1))
                    sp.wait_ge(s_natact, s * TS + (k + 1))
                    sp.dma_start(nat[k % 2], adj[bass.ds(s * SW + k * P, P), :]).then_inc(s_nat[k % 2], 16)
                    sp.wait_ge(s_piece, s * PIECES + (k + 1))
                    apart(sp, s_psp)
                    sp.dma_start(adjT_sb[:, k], adj_t[k * JT * P:(k + 1) * JT * P, bass.ds(s * SW, SW)]
                                 .rearrange("(j p) i -> p j i", p=P)).then_inc(s_adjT[k], 16)
                    if k == 1:
                        sp.wait_ge(s_ns, s)
                        sp.dma_start(xTs, x_t[:, bass.ds(s * SW, SW)]).then_inc(s_xT, 16)

            sp.wait_ge(s_ctl, 1)
            for b in range(2):
                sp.wait_ge(s_rows[b], 2 * 16 * T // 2)
            nblk = ctl_value(sp, CTL_NB, 1, NBLK)
            gen = ctl_value(sp, CTL_GEN, 0, 1)
            with sp.Fori(0, T // 2) as tt:
                for u in range(2):
                    t = tt * 2 + u
                    sp.wait_ge(s_tdve, tt * 2 + (u + 1))
                    sp.dma_start(xi_sb[u], table_i[bass.ds(tt * (2 * P) + u * P, P), :]).then_inc(s_xi[u], 16)
                    with sp.If(gen > 0):
                        before_a = ctl_value(sp, tt * 2 + (u + CTL_A0), 0, MAXN)
                        before_b = ctl_value(sp, tt * 2 + (u + CTL_B0), 0, MAXN)
                        with sp.Fori(0, nblk) as blk:
                            for b, before in ((0, before_a), (1, before_b)):
                                sp.wait_ge(s_xv[b], before + blk * TURNS)
                                sp.wait_ge(s_idx[b], before + blk * TURNS)
                                apart(sp, s_psp)
                            sp.dma_start(slot_val[:, bass.ds(tt * (2 * BLOCK) + u * BLOCK, BLOCK)],
                                         adj[bass.ds(tt * (2 * P) + u * P, P), bass.ds(blk * BLOCK, BLOCK)]
                                         ).then_inc(s_blk, 16)
                            sp.dma_start(slot_idx[:, bass.ds(tt * (2 * BLOCK) + u * BLOCK, BLOCK)],
                                         columns[:, bass.ds(blk * BLOCK, BLOCK)].to_broadcast((P, BLOCK))
                                         ).then_inc(s_blk, 16)
                        sp.nop()
                    sp.nop()

            with sp.Fori(0, STRIPS) as s:
                sp.wait_ge(s_oC, s + 1)
                sp.dma_start(out[bass.ds(s * SW, SW), :].rearrange("(k p) d -> p k d", p=P),
                             oC.rearrange("p (k d) -> p k d", k=TS)).then_inc(s_out, 16)
            sp.wait_ge(s_out, 16 * STRIPS)

        @block.gpsimd
        def _(pool):
            nc.gpsimd.memset(ident[:, :], 0.0).then_inc(s_ident, 1)
            pool.wait_ge(s_ident, 1)
            nc.gpsimd.affine_select(out=ident[:, :], in_=ident[:, :], compare_op=ALU.not_equal, fill=1.0, base=0,
                                    pattern=[[-1, P]], channel_multiplier=1).then_inc(s_ident, 1)
            with pool.Fori(0, STRIPS) as s:
                pool.wait_ge(s_xp, s + 1)
                nc.gpsimd.tensor_copy(xp_all[:, bass.ds(s * TS, TS), :],
                                      xpA.rearrange("p (k d) -> p k d", k=TS)).then_inc(s_xpall, 1)
                for k in range(TS):
                    b = k % 2
                    pool.wait_ge(s_rows[b], s * (2 * 32) + (k // 2) * 32)
                    apart(pool, s_ppool)
                    nc.gpsimd.tensor_copy(row_j[b][:, ZW:ZW + D], xpA[:, k * D:(k + 1) * D]).then_inc(s_rx, 1)
                    pool.wait_ge(s_rx, s * TS + (k + 1))
                    pool.wait_ge(s_12c, s * TS + (k + 1))
                    pool.dma_start(table_j[bass.ds(s * SW + k * P, P), :], row_j[b]).then_inc(s_rows[b], 16)
                    pool.dma_start(table_i[bass.ds(s * SW + k * P, P), :], row_i[b]).then_inc(s_rows[b], 16)

            for b in range(2):
                pool.wait_ge(s_rows[b], 2 * 16 * T // 2)
            pool.wait_ge(s_ctl, 1)
            nblk = ctl_value(pool, CTL_NB, 1, NBLK)
            gen = ctl_value(pool, CTL_GEN, 0, 1)

            def gather(b, n, slot):
                pool.wait_ge(s_z[b], n)
                pool.wait_ge(s_xv[b], n)
                apart(pool, s_ppool)
                nc.gpsimd.tensor_copy(idx_sb[b], slot_idx[:, bass.ds(slot, G)]).then_inc(s_idx[b], 1)
                pool.wait_ge(s_idx[b], n + 1)
                apart(pool, s_ppool)
                for r in range(G):
                    nc.gpsimd.indirect_dma_start(
                        g_sb[b][:, r, :], None, table_j,
                        bass.IndirectOffsetOnAxis(ap=idx_sb[b][:, r:r + 1], axis=0)).then_inc(s_g[b], 16)

            with pool.Fori(0, T) as t:
                turns_a, turns_b, before_a, before_b = tile_counts(pool, t)
                with pool.Fori(0, nblk) as blk:
                    with pool.If(gen > 0):
                        pool.wait_ge(s_blk, t * (32 * NBLK) + blk * 32 + 32)
                        pool.nop()
                    with pool.Fori(0, turns_a) as i:
                        gather(0, before_a + blk * TURNS + i, t * BLOCK + i * (2 * G))
                        with pool.If(i < turns_b):
                            gather(1, before_b + blk * TURNS + i, t * BLOCK + i * (2 * G) + G)
                            pool.nop()
                        pool.nop()

        @block.vector
        def _(dve):
            v = nc.vector
            chain = [0, 0]

            def link(ins):
                ins.then_inc(s_chain, 1)
                chain[0] += 1

            def settle(alone=False):
                dve.wait_ge(s_chain, chain[1] * LINKS + chain[0])
                if alone:
                    apart(dve, s_pdve)

            dve.sem_inc(s_natdve, 2)
            dve.sem_inc(s_tdve, 2)
            dve.sem_inc(s_evac, 2)
            v.memset(eps[:, :], EPS).then_inc(s_const, 1)
            for b in range(2):
                v.memset(row_j[b][:, ROWJ - 1:ROWJ], 1.0).then_inc(s_const, 1)
            dve.wait_ge(s_w, 16 * LOADS)
            v.tensor_scalar(a_bc[:, :], a_bc[:, :], POS, None, ALU.mult).then_inc(s_abc, 1)
            dve.wait_ge(s_v, 1)
            v.tensor_scalar(v1_sb[:, :], b_pq[:, 0:H], LIN, None, ALU.mult).then_inc(s_vsb, 1)
            v.tensor_scalar(v2_sb[:, :], b_pq[:, H:2 * H], LIN, None, ALU.mult).then_inc(s_vsb, 1)

            LINKS = 89
            with dve.Fori(0, STRIPS) as s:
                chain[:] = [0, s]
                for k in range(TS):
                    b = k % 2
                    dve.wait_ge(s_nat[b], s * 32 + 16 * (k // 2 + 1))
                    apart(dve, s_pdve)
                    for c in range(NCH):
                        last = v.max(cand[b][:, 8 * c:8 * c + 8], nat[b][:, c * CH:(c + 1) * CH])
                    link(last)
                    settle(alone=True)
                    for c in range(NCH):
                        last = v.max_index(cand_i[b][:, 8 * c:8 * c + 8], cand[b][:, 8 * c:8 * c + 8],
                                           nat[b][:, c * CH:(c + 1) * CH])
                    last.then_inc(s_natdve, 1)
                    link(v.scalar_tensor_tensor(keep, cand[b], 0.0, lane_sb, ALU.is_gt, ALU.mult))
                    link(v.tensor_scalar(part[0], cand[b].bitcast(I32), 16, None, ALU.logical_shift_right))
                    link(v.tensor_scalar(part[1], cand[b].bitcast(I32), 0xffff, None, ALU.bitwise_and))
                    dve.wait_ge(s_natdve, s * TS + (k + 3))
                    link(v.scalar_tensor_tensor(comp[b][2], cand[b], 0.0, cand_i[b], ALU.is_gt, ALU.mult))
                    settle()
                    link(v.tensor_tensor(comp[b][0], keep, part[0], ALU.add))
                    link(v.tensor_tensor(comp[b][1], keep, part[1], ALU.add))
                    link(v.tensor_tensor(comp[b][2], keep, comp[b][2], ALU.add))
                    settle(alone=True)
                    for r in range(ROUNDS):
                        for c in range(3):
                            last = v.max(best[:, c, k, 8 * r:8 * r + 8], comp[b][c])
                        link(last)
                        if r < ROUNDS - 1:
                            settle(alone=True)
                            for c in range(3):
                                last = v.match_replace(comp[b][c], best[:, c, k, 8 * r:8 * r + 8], comp[b][c], 0.0)
                            link(last)
                            settle(alone=True)
                settle()
                for c in range(3):
                    last = v.tensor_scalar(dec[:, c], best[:, c], 1.0, 0.0, ALU.subtract, ALU.max)
                link(last)
                settle()
                link(v.tensor_scalar(best[:, 0].bitcast(I32), dec[:, 0], 0xffff, 16, ALU.bitwise_and,
                                     ALU.logical_shift_left))
                link(v.tensor_scalar(best[:, 1].bitcast(I32), dec[:, 1], 0xffff, None, ALU.bitwise_and))
                link(v.tensor_scalar(best[:, 2].bitcast(I32), dec[:, 2], KEY + 3, 8, ALU.logical_shift_right,
                                     ALU.logical_shift_left))
                link(v.tensor_scalar(dec_i, dec[:, 2], CH - 1, None, ALU.bitwise_and))
                settle()
                at_val = slot_val[:, bass.ds(s * (TS * BLOCK), TS * BLOCK)].rearrange("p (k s) -> p k s", k=TS)
                at_idx = slot_idx[:, bass.ds(s * (TS * BLOCK), TS * BLOCK)].rearrange("p (k s) -> p k s", k=TS)
                link(v.tensor_tensor(at_val[:, :, 0:SLOTS].bitcast(I32), best[:, 0].bitcast(I32),
                                     best[:, 1].bitcast(I32), ALU.bitwise_or))
                link(v.tensor_tensor(at_idx[:, :, 0:SLOTS], best[:, 2].bitcast(I32), dec_i,
                                     ALU.bitwise_or))
                settle()
                link(v.tensor_scalar(best[:, 0], at_val[:, :, 0:SLOTS], 0.0, None, ALU.is_gt))
                settle()
                link(v.tensor_reduce(found[:, bass.ds(s * TS, TS)], best[:, 0], AX, ALU.add))

                dve.wait_ge(s_natact, s * TS + (TS + 2))
                link(v.tensor_scalar(rdeg, deg_all[:, bass.ds(s * TS, TS)], 1.0, None, ALU.max))
                settle()
                link(v.reciprocal(rdeg, rdeg))
                settle()
                dve.wait_ge(s_ns, s + 1)
                for k in range(TS):
                    link(v.scalar_tensor_tensor(yA[:, k * D:(k + 1) * D], b_n[:, k * D:(k + 1) * D],
                                                rdeg[:, k:k + 1], h_sb[:, s * TS + k, :], ALU.mult, ALU.add))
                settle()
                link(v.tensor_tensor(yA, yA, b_s[:, :], ALU.add))
                settle()
                for k in range(TS):
                    link(v.bn_stats(stat[:, k, :], yA[:, k * D:(k + 1) * D]))
                settle(alone=True)
                for k in range(TS):
                    last = v.bn_aggr(mv[:, k, :], stat[:, k, :])
                last.then_inc(s_var, 1)
                dve.wait_ge(s_std, s + 1)
                link(v.reciprocal(rstd, rstd))
                settle()
                dve.wait_ge(s_xpTps, s)
                dve.wait_ge(s_xpall, s)
                dve.wait_ge(s_rx, s * TS)
                for k in range(TS):
                    last = v.tensor_scalar(xpA[:, k * D:(k + 1) * D], yA[:, k * D:(k + 1) * D], mv[:, k, 0:1],
                                           rstd[:, k:k + 1], ALU.subtract, ALU.mult)
                last.then_inc(s_xp, 1)
                assert chain[0] == LINKS, chain

            c = [0]

            def step(ins):
                ins.then_inc(s_cC, 1)
                c[0] += 1
                dve.wait_ge(s_cC, c[0])

            dve.wait_ge(s_chain, STRIPS * LINKS)
            step(v.tensor_tensor(both[:, T:], found, cnt_all, ALU.subtract))
            step(v.tensor_tensor(both[:, T:], both[:, T:], both[:, T:], ALU.mult))
            step(v.tensor_tensor(both[:, T:], both[:, T:], neg_all, ALU.add))
            step(v.tensor_copy(both[:, 0:T], cnt_all))
            dve.wait_ge(s_bothT, 1)
            v.tensor_reduce(peak[0:2 * T, :], b_ctl[0:2 * T, 0:P], AX, ALU.max).then_inc(s_peak, 1)
            dve.wait_ge(s_peakT, 1)
            R = [crow[0:1, i * T:(i + 1) * T] for i in range(8)]
            I = [irow[0:1, i * T:(i + 1) * T] for i in range(4)]
            step(v.tensor_copy(crow[0:1, 0:2 * T], b_ctl[0:1, 256:256 + 2 * T]))
            gen, one = R[2][:, 0:1], R[3]
            step(v.tensor_reduce(gen, R[1], AX, ALU.max))
            step(v.tensor_scalar(gen, gen, 0.0, None, ALU.is_gt))
            step(v.tensor_scalar(I[0], R[0], float(G - 1), float(BLOCK), ALU.add, ALU.min))
            step(v.tensor_scalar(I[0], I[0], 2, None, ALU.logical_shift_right))
            step(v.tensor_copy(R[3], I[0]))
            step(v.tensor_scalar(R[3], R[3], 1.0, None, ALU.max))
            step(v.tensor_scalar(R[4], R[3], -1.0, float(BLOCK // G), ALU.mult, ALU.add))
            step(v.scalar_tensor_tensor(R[3], R[4], gen, R[3], ALU.mult, ALU.add))
            step(v.tensor_copy(I[1], R[3]))
            step(v.tensor_scalar(I[0], R[3], 1.0, None, ALU.add))
            step(v.tensor_scalar(ctl[0:1, CTL_A:CTL_A + T], I[0], 1, None, ALU.logical_shift_right))
            step(v.tensor_scalar(ctl[0:1, CTL_B:CTL_B + T], I[1], 1, None, ALU.logical_shift_right))
            step(v.tensor_scalar(R[2][:, 1:2], gen, float(NBLK - 1), 1.0, ALU.mult, ALU.add))
            step(v.tensor_copy(ctl[0:1, CTL_GEN:CTL_GEN + 1], gen))
            step(v.tensor_copy(ctl[0:1, CTL_NB:CTL_NB + 1], R[2][:, 1:2]))
            step(v.memset(R[7], 1.0))
            for at, to in ((CTL_A, CTL_A0), (CTL_B, CTL_B0)):
                step(v.tensor_scalar(R[4], ctl[0:1, at:at + T], R[2][:, 1:2], None, ALU.mult))
                step(v.tensor_tensor_scan(R[5], R[7], R[4], 0.0, ALU.mult, ALU.add))
                last = v.tensor_tensor(ctl[0:1, to:to + T], R[5], R[4], ALU.subtract)
                if to == CTL_A0:
                    step(last)
            last.then_inc(s_ctl, 1)
            dve.wait_ge(s_ctl, 1)

            for b in range(2):
                dve.wait_ge(s_rows[b], 2 * 16 * T // 2)
            v.memset(zeros, 0.0).then_inc(s_zero, 1)
            nblk = ctl_value(dve, CTL_NB, 1, NBLK)

            def score(b, n, u):
                dve.wait_ge(s_g[b], n * (16 * G) + 16 * G)
                v.tensor_tensor(z_sb[b], g_sb[b][:, :, 0:ZW], xi_sb[u].rearrange("p (o c) -> p o c", o=1)
                                .to_broadcast((P, G, ZW)), ALU.add).then_inc(s_z[b], 1)
                dve.wait_ge(s_z[b], n + 1)
                dve.wait_ge(s_th[b], n)
                for r in range(G):
                    for h in range(H):
                        last = v.scalar_tensor_tensor(z_sb[b][:, r, h * D:(h + 1) * D],
                                                      z_sb[b][:, r, h * D:(h + 1) * D], 0.0,
                                                      a_bc[:, h * D:(h + 1) * D], ALU.max, ALU.mult,
                                                      accum_out=sc_sb[b][:, r * H + h:r * H + h + 1])
                last.then_inc(s_acc[b], 1)
                dve.wait_ge(s_acc[b], n + 1)
                sc = sc_sb[b].rearrange("p (r h) -> p r h", r=G)
                v.tensor_tensor(sc, sc, z_sb[b][:, :, HD:ZW], ALU.add).then_inc(s_sc[b], 1)

            def evacuate(t, u):
                dve.wait_ge(s_tpe, t + 1)
                v.tensor_copy(agg_all[:, t, :], agg_ps[u][:, :])
                v.tensor_copy(z_all[:, t, :], z_ps[u][:, 0:H]).then_inc(s_evac, 1)

            def score_tile(t, u, xi_count):
                turns_a, turns_b, before_a, before_b = tile_counts(dve, t)
                dve.wait_ge(s_xi[u], xi_count)
                apart(dve, s_pdve)
                with dve.Fori(0, nblk) as blk:
                    with dve.Fori(0, turns_a) as i:
                        score(0, before_a + blk * TURNS + i, u)
                        with dve.If(i < turns_b):
                            score(1, before_b + blk * TURNS + i, u)
                            dve.nop()
                        dve.nop()
                dve.drain().then_inc(s_tdve, 1)

            score_tile(0, 0, 16)
            with dve.Fori(0, T // 2 - 1) as tt:
                for u in (1, 0):
                    score_tile(tt * 2 + (2 - u), u, tt * 16 + (16 if u else 32))
                    evacuate(tt * 2 + (1 - u), 1 - u)
            score_tile(T - 1, 1, T // 2 * 16)
            evacuate(T - 2, 0)
            evacuate(T - 1, 1)

            dve.wait_ge(s_evac, T + 2)
            LC = 4
            c0 = c[0]
            with dve.Fori(0, STRIPS) as s:
                n = [0]

                def step(ins):
                    ins.then_inc(s_cC, 1)
                    n[0] += 1
                    dve.wait_ge(s_cC, s * LC + (c0 + n[0]))

                step(v.reciprocal(rzC, z_all[:, bass.ds(s * TS, TS), :]))
                dve.wait_ge(s_aTps, s * H)
                for k in range(TS):
                    for h in range(H):
                        last = v.tensor_scalar(aggn[:, k, h * D:(h + 1) * D],
                                               agg_all[:, s * TS + k, h * D:(h + 1) * D],
                                               rzC[:, k * H + h:k * H + h + 1], None, ALU.mult)
                last.then_inc(s_aggn, 1)
                for h in range(H):
                    dve.wait_ge(s_linc, s * H + (h + 1))
                    if h == 0:
                        dve.wait_ge(s_o, s)
                    v.scalar_tensor_tensor(yleak[:, h, :], lin_ps[h][:, :], SLOPE, ylin[:, h, :], ALU.mult,
                                           ALU.max).then_inc(s_leak, 1)
                dve.wait_ge(s_o, s + 1)
                step(v.tensor_tensor(yC, bO_ps[:, :], xp_all[:, bass.ds(s * TS, TS), :].rearrange("p k d -> p (k d)"),
                                     ALU.add))
                for k in range(TS):
                    last = v.bn_stats(statC[:, k, :], yC[:, k * D:(k + 1) * D])
                step(last)
                apart(dve, s_pdve)
                for k in range(TS):
                    last = v.bn_aggr(mvC[:, k, :], statC[:, k, :])
                last.then_inc(s_varC, 1)
                dve.wait_ge(s_stdC, s + 1)
                step(v.reciprocal(rstdC, rstdC))
                dve.wait_ge(s_out, s * 16)
                for k in range(TS):
                    last = v.tensor_scalar(oC[:, k * D:(k + 1) * D], yC[:, k * D:(k + 1) * D], mvC[:, k, 0:1],
                                           rstdC[:, k:k + 1], ALU.subtract, ALU.mult)
                last.then_inc(s_oC, 1)
                assert n[0] == LC, n

        @block.scalar
        def _(act):
            a = nc.scalar
            act.sem_inc(s_natact, 2)
            act.wait_ge(s_const, 3)
            with act.Fori(0, STRIPS) as s:
                for k in range(TS):
                    b = k % 2
                    act.wait_ge(s_nat[b], s * 32 + 16 * (k // 2 + 1))
                    act.wait_ge(s_natact, s * TS + (k + 2))
                    a.activation(junk, nat[b], ACT.Copy,
                                 accum_out=deg_all[:, bass.ds(s * TS + k, 1)]).then_inc(s_pass, 1)
                    act.wait_ge(s_pass, s * (2 * TS) + (2 * k + 1))
                    a.activation(junk, nat[b], ACT.Sign,
                                 accum_out=cnt_all[:, bass.ds(s * TS + k, 1)]).then_inc(s_pass, 1)
                    act.wait_ge(s_pass, s * (2 * TS) + (2 * k + 2))
                    a.activation(junk, nat[b], ACT.Relu, scale=-1.0,
                                 accum_out=neg_all[:, bass.ds(s * TS + k, 1)]).then_inc(s_natact, 1)
                act.wait_ge(s_piece, s * PIECES + 2 * PIECES)
                act.wait_ge(s_ns, s)
                a.activation(aggT, b_aggT[:, :], ACT.Copy).then_inc(s_aggT, 1)
                act.wait_ge(s_var, s + 1)
                a.activation(rstd, mv[:, :, 1:2], ACT.Sqrt, bias=eps[:, 0:1]).then_inc(s_std, 1)
                act.wait_ge(s_xpTps, s + 1)
                act.wait_ge(s_12, s * TS)
                a.activation(xpT, b_x[:, :], ACT.Copy).then_inc(s_xpT, 1)
                for k in range(TS):
                    b = k % 2
                    act.wait_ge(s_12, s * TS + (k + 1))
                    act.wait_ge(s_rows[b], s * (2 * 32) + (k // 2) * 32)
                    a.activation(row_j[b][:, 0:HD], b_2[:, :], ACT.Copy)
                    a.activation(row_j[b][:, HD:ZW], b_pq[:, H:2 * H], ACT.Copy)
                    a.activation(row_i[b][:, HD:ZW], b_pq[:, 0:H], ACT.Copy)
                    a.activation(row_i[b][:, 0:HD], b_1[:, :], ACT.Copy).then_inc(s_12c, 1)

            act.wait_ge(s_ctl, 1)
            nblk = ctl_value(act, CTL_NB, 1, NBLK)

            def weigh(b, n, slot):
                act.wait_ge(s_g[b], n * (16 * G) + 16 * G)
                act.wait_ge(s_sx[b], n)
                for r in range(G):
                    last = a.activation(xv_sb[b][:, r, :], g_sb[b][:, r, ZW:ROWJ], ACT.Copy,
                                        scale=slot_val[:, bass.ds(slot + r, 1)])
                last.then_inc(s_xv[b], 1)
                act.wait_ge(s_sc[b], n + 1)
                a.activation(th_sb[b], sc_sb[b], ACT.Tanh, scale=0.125).then_inc(s_th[b], 1)
                act.wait_ge(s_th[b], n + 1)
                a.activation(e_sb[b], th_sb[b], ACT.Exp, scale=8.0).then_inc(s_e[b], 1)
                act.wait_ge(s_e[b], n + 1)
                act.wait_ge(s_xv[b], n + 1)
                act.wait_ge(s_sum[b], n)
                for r in range(G):
                    for h in range(H):
                        last = a.activation(sx_sb[b][:, r, h, :], xv_sb[b][:, r, :], ACT.Copy,
                                            scale=e_sb[b][:, r * H + h:r * H + h + 1])
                last.then_inc(s_sx[b], 1)

            with act.Fori(0, T) as t:
                turns_a, turns_b, before_a, before_b = tile_counts(act, t)
                with act.Fori(0, nblk) as blk:
                    with act.Fori(0, turns_a) as i:
                        weigh(0, before_a + blk * TURNS + i, t * BLOCK + i * (2 * G))
                        with act.If(i < turns_b):
                            weigh(1, before_b + blk * TURNS + i, t * BLOCK + i * (2 * G) + G)
                            act.nop()
                        act.nop()

            with act.Fori(0, STRIPS) as s:
                for h in range(H):
                    act.wait_ge(s_aTps, s * H + (h + 1))
                    if h == 0:
                        act.wait_ge(s_lin, s * H)
                    a.activation(aggnT[:, h, :], bT_ps[h % 2][:, :], ACT.Copy).then_inc(s_aT, 1)
                for h in range(H):
                    act.wait_ge(s_lin, s * H + (h + 1))
                    if h == 0:
                        act.wait_ge(s_leak, s * H)
                    a.activation(ylin[:, h, :], lin_ps[h][:, :], ACT.Copy).then_inc(s_linc, 1)
                act.wait_ge(s_varC, s + 1)
                a.activation(rstdC, mvC[:, :, 1:2], ACT.Sqrt, bias=eps[:, 0:1]).then_inc(s_stdC, 1)

        @block.tensor
        def _(pe):
            mm = nc.tensor.matmul
            pe.sem_inc(s_piece, PIECES)
            pe.wait_ge(s_w, 16 * LOADS)
            for w in range(2):
                for h in range(H):
                    last = mm(b_pq[:, w * H + h:w * H + h + 1], w12t[:, w, h, :], acol_sb[:, h:h + 1],
                              start=True, stop=True)
            last.then_inc(s_v, 1)
            pe.wait_ge(s_ident, 2)
            pe.wait_ge(s_vsb, 2)
            with pe.Fori(0, STRIPS) as s:
                pe.wait_ge(s_aggT, s)
                for q in range(PIECES):
                    pe.wait_ge(s_adjT[q], s * 16 + 16)
                    for j in range(JT):
                        jt = q * JT + j
                        last = mm(b_aggT[:, :], h_sb[:, jt, :], adjT_sb[:, q, j, :], start=jt == 0, stop=jt == T - 1)
                    last.then_inc(s_piece, 1)
                pe.wait_ge(s_aggT, s + 1)
                pe.wait_ge(s_xT, s * 16 + 16)
                for k in range(TS):
                    mm(b_n[:, k * D:(k + 1) * D], aggT[:, k * P:(k + 1) * P], wneigh_sb[:, :], start=True, stop=True)
                    last = mm(b_s[:, k * D:(k + 1) * D], xTs[:, k * P:(k + 1) * P], wself_sb[:, :], start=True,
                              stop=True)
                last.then_inc(s_ns, 1)
                pe.wait_ge(s_xp, s + 1)
                pe.wait_ge(s_xpT, s)
                for k in range(TS):
                    last = nc.tensor.transpose(b_x[:, k * P:(k + 1) * P], xpA[:, k * D:(k + 1) * D], ident[:, :])
                last.then_inc(s_xpTps, 1)
                pe.wait_ge(s_xpT, s + 1)
                for k in range(TS):
                    pe.wait_ge(s_12c, s * TS + k)
                    xk = xpT[:, k * P:(k + 1) * P]
                    mm(b_1[:, :], xk, w1_sb[:, :, :].rearrange("p h k -> p (h k)"), start=True, stop=True)
                    mm(b_2[:, :], xk, w2_sb[:, :, :].rearrange("p h k -> p (h k)"), start=True, stop=True)
                    mm(b_pq[:, 0:H], xk, v1_sb[:, :], start=True, stop=True)
                    mm(b_pq[:, H:2 * H], xk, v2_sb[:, :], start=True, stop=True).then_inc(s_12, 1)

            pe.wait_ge(s_cC, 4)
            nc.tensor.transpose(b_ctl[0:2 * T, 0:P], both, ident[:, :]).then_inc(s_bothT, 1)
            pe.wait_ge(s_peak, 1)
            mm(b_ctl[0:1, 256:256 + 2 * T], peak[0:2 * T, :], ident[0:2 * T, 0:2 * T], start=True,
               stop=True).then_inc(s_peakT, 1)
            pe.wait_ge(s_ctl, 1)
            pe.wait_ge(s_12c, T)
            pe.wait_ge(s_zero, 1)
            nblk = ctl_value(pe, CTL_NB, 1, NBLK)

            def add_up(b, n, u):
                pe.wait_ge(s_sx[b], n + 1)
                for r in range(G):
                    mm(agg_ps[u][:, :], ident[:, :], sx_sb[b][:, r, :, 0:D], start=False, stop=False)
                    last = mm(z_ps[u][:, 0:H], ident[:, :], sx_sb[b][:, r, :, D:XW], start=False, stop=False)
                last.then_inc(s_sum[b], 1)

            with pe.Fori(0, T // 2) as tt:
                for u in range(2):
                    turns_a, turns_b, before_a, before_b = tile_counts(pe, tt * 2 + u)
                    pe.wait_ge(s_evac, tt * 2 + (u + 1))
                    mm(agg_ps[u][:, :], ident[:, :], zeros, start=True, stop=False)
                    mm(z_ps[u][:, 0:H], ident[:, :], zeros[:, 0:H], start=True, stop=False)
                    with pe.Fori(0, nblk) as blk:
                        with pe.Fori(0, turns_a) as i:
                            add_up(0, before_a + blk * TURNS + i, u)
                            with pe.If(i < turns_b):
                                add_up(1, before_b + blk * TURNS + i, u)
                                pe.nop()
                            pe.nop()
                    mm(agg_ps[u][:, :], ident[:, :], zeros, start=False, stop=True)
                    mm(z_ps[u][:, 0:H], ident[:, :], zeros[:, 0:H], start=False, stop=True).then_inc(s_tpe, 1)

            with pe.Fori(0, STRIPS) as s:
                pe.wait_ge(s_aggn, s + 1)
                for h in range(H):
                    pe.wait_ge(s_aT, s * H + max(h - 1, 0))
                    for k in range(TS):
                        last = nc.tensor.transpose(bT_ps[h % 2][:, k * P:(k + 1) * P],
                                                   aggn[:, k, h * D:(h + 1) * D], ident[:, :])
                    last.then_inc(s_aTps, 1)
                pe.wait_ge(s_leak, s * H)
                for h in range(H):
                    pe.wait_ge(s_aT, s * H + (h + 1))
                    mm(lin_ps[h][:, :], wlin_sb[:, h, :], aggnT[:, h, :], start=True, stop=True).then_inc(s_lin, 1)
                pe.wait_ge(s_leak, s * H + H)
                for k in range(TS):
                    for h in range(H):
                        last = mm(bO_ps[:, k * D:(k + 1) * D], yleak[:, h, k * P:(k + 1) * P], wout_sb[:, h, :],
                                  start=h == 0, stop=h == H - 1)
                last.then_inc(s_o, 1)


def kernel(x, adj, L0_gnn_W_self, L0_gnn_W_neigh, L1_gnn_w1, L1_gnn_w2, L1_gnn_a, L1_gnn_Wlin, L1_gnn_w):
    import numpy as np
    import concourse.bacc as bacc
    from concourse import mybir as mb
    from concourse.bass_utils import run_bass_kernel_spmd

    x, adj, a = np.asarray(x), np.asarray(adj), np.asarray(L1_gnn_a)
    w1, w2, wlin = np.asarray(L1_gnn_w1), np.asarray(L1_gnn_w2), np.asarray(L1_gnn_Wlin)
    n, d = x.shape
    candidates = n // 256 * 8
    arrays = {
        "x": x, "x_t": x.T, "adj": adj, "adj_t": adj.T,
        "w_self": np.asarray(L0_gnn_W_self), "w_neigh": np.asarray(L0_gnn_W_neigh),
        "w1": w1, "w2": w2, "w1_t": w1.transpose(0, 2, 1), "w2_t": w2.transpose(0, 2, 1),
        "a_row": a.reshape(1, -1), "a_col": a.T, "wlin_t": wlin.transpose(0, 2, 1), "w_out": np.asarray(L1_gnn_w),
        "lane": (np.arange(candidates) * 2.0 ** 17 + 1).astype(np.float32)[None, :],
        "columns": np.arange(n, dtype=np.int32)[None, :],
    }
    arrays = {k: np.ascontiguousarray(v) for k, v in arrays.items()}
    nc = bacc.Bacc("TRN2", target_bir_lowering=False, num_devices=1)
    args = {k: nc.dram_tensor(k, v.shape, mb.dt.from_np(v.dtype), kind="ExternalInput").ap()
            for k, v in arrays.items()}
    out = nc.dram_tensor("out", (n, d), mb.dt.float32, kind="ExternalOutput").ap()
    two_layer_graph_kernel(nc, **args, out=out)
    r = run_bass_kernel_spmd(nc, [arrays], core_ids=[0])
    return r.results[0]["out"]
```

```python
import concourse.bass as bass
from concourse import mybir
from contextlib import ExitStack


def two_layer_graph_kernel(nc, x, x_t, adj, adj_t, w_self, w_neigh, w1, w2, w1_t, w2_t, a_row, a_col,
                           wlin_t, w_out, lane, columns, bins, ends, out):
    F32, I32, U32 = mybir.dt.float32, mybir.dt.int32, mybir.dt.uint32
    BF16 = mybir.dt.bfloat16
    ALU = mybir.AluOpType
    ACT = mybir.ActivationFunctionType
    AX = mybir.AxisListType.X

    P = 128
    N, D = x.shape
    H = w1.shape[0]
    HD = H * D
    T = N // P
    TS = 4
    STRIPS = T // TS
    SW = TS * P
    PIECES = 4
    JT = T // PIECES
    CH = 256
    NCH = N // CH
    CAND = 8 * NCH
    ROUNDS = 5
    SLOTS = 8 * ROUNDS
    BLOCK = 64
    NBLK = N // BLOCK
    G = 4
    HALVES = 2
    TURNS = BLOCK // G // HALVES
    KEY = 17
    ROWJ = HD + H + D + 1
    ROWI = HD + H + D
    REC = 2 * BLOCK + 1
    IDX, NUM, VAL = 0, BLOCK, BLOCK + 1
    BINS = 64
    ZW = HD + H
    XW = D + 1
    EPS = 1e-5
    SLOPE = 0.01
    LOADS = 14
    LIN = SLOPE
    POS = 1 - SLOPE

    table_j = nc.dram_tensor("table_j", [N, ROWJ], F32, kind="Internal").ap()
    records = nc.dram_tensor("records", [N, REC], I32, kind="Internal").ap()
    table_i = nc.dram_tensor("table_i", [N, ROWI], F32, kind="Internal").ap()

    ctx = ExitStack()
    with ctx:
        def sb(name, shape, dt=F32):
            return ctx.enter_context(nc.sbuf_tensor(name, shape, dt))

        def ps(name, shape):
            return ctx.enter_context(nc.psum_tensor(name, shape, F32))

        def sem(name):
            return ctx.enter_context(nc.semaphore(name))

        ident = sb("ident", [P, P])
        ones_h = sb("ones_h", [P, P], BF16)
        before_h = sb("before_h", [P, P], BF16)
        ones_f = sb("ones_f", [P, P])
        xs_all = sb("xs_all", [P, T, D])
        num_all = sb("num_all", [P, T], I32)
        rec_all = sb("rec_all", [P, T, REC], I32)
        pos_all = sb("pos_all", [P, T], I32)
        ctl = sb("ctl", [1, 6 * T + 2], I32)
        a_bc = sb("a_bc", [P, HD])
        wlin_sb = sb("wlin_sb", [P, H, D])
        wout_sb = sb("wout_sb", [P, H, D])
        wself_sb = sb("wself_sb", [P, D])
        wneigh_sb = sb("wneigh_sb", [P, D])
        w1_sb = sb("w1_sb", [P, H, D])
        w2_sb = sb("w2_sb", [P, H, D])
        v1_sb = sb("v1_sb", [P, H])
        v2_sb = sb("v2_sb", [P, H])
        big = sb("big", [P, PIECES * JT * SW])
        adjT_sb = big[:, :].rearrange("p (q j i) -> p q j i", q=PIECES, j=JT)
        agg_all = big[:, :].rearrange("p (t c) -> p t c", t=T)
        z_all = sb("z_all", [P, T, H])
        AREA = 24 * 1024
        area = sb("area", [P, AREA])
        used = [0]

        def cut(n, dt=F32):
            at = used[0]
            used[0] += n
            assert used[0] <= AREA, used[0]
            v = area[:, at:at + n]
            return v if dt is F32 else v.bitcast(dt)

        nat = [cut(N) for _ in range(2)]
        junk = cut(N // 2, BF16)
        h_sb = cut(T * D).rearrange("p (t d) -> p t d", t=T)
        xTs = cut(SW)
        aggT = cut(SW)
        xpT = cut(SW)
        cand = [cut(CAND) for _ in range(2)]
        cand_i = [cut(CAND, U32) for _ in range(2)]
        keep = cut(CAND)
        comp = [[cut(CAND) for _ in range(3)] for _ in range(2)]
        part = [cut(CAND, I32) for _ in range(3)]
        best = cut(3 * TS * SLOTS).rearrange("p (c k s) -> p c k s", c=3, k=TS)
        dec = cut(3 * TS * SLOTS, I32).rearrange("p (c k s) -> p c k s", c=3, k=TS)
        dec_i = cut(TS * SLOTS, I32).rearrange("p (k s) -> p k s", k=TS)
        lane_sb = cut(CAND)
        row_j = [cut(ROWJ) for _ in range(2)]
        row_i = [cut(ROWI) for _ in range(2)]
        yA = cut(SW)
        xpA = cut(SW)
        stat = cut(TS * 6).rearrange("p (k c) -> p k c", k=TS)
        mv = cut(TS * 2).rearrange("p (k c) -> p k c", k=TS)
        rstd = cut(TS)
        rdeg = cut(TS)
        deg_all = cut(T)
        cnt_all = cut(T)
        neg_all = cut(T)
        found = cut(T)
        acol_sb = cut(H)
        w12t = cut(2 * HD).rearrange("p (w h c) -> p w h c", w=2, h=H)
        crow = cut(8 * T)
        irow = cut(4 * T, I32)
        staged_at = used[0]
        bins_sb = cut(BINS)
        ends_sb = cut(T)
        gen_sb = cut(4)
        bad = cut(T)
        stage = [cut(REC, I32) for _ in range(2)]
        stage_pos = [cut(1, I32) for _ in range(2)]
        NB_ = T * BINS
        total = nat[0][:, 0:NB_].rearrange("p (b t) -> p b t", b=BINS)
        upto = nat[0][:, NB_:2 * NB_].rearrange("p (b t) -> p b t", b=BINS)
        place = nat[1][:, 0:NB_].rearrange("p (t b) -> p t b", t=T)
        onehot = nat[1][:, NB_:NB_ + NB_ // 2].bitcast(BF16).rearrange("p (t b) -> p t b", t=T)

        used[0] = 0
        g_sb = [cut(G * ROWJ).rearrange("p (r c) -> p r c", r=G) for _ in range(HALVES)]
        z_sb = [cut(G * ZW).rearrange("p (r c) -> p r c", r=G) for _ in range(HALVES)]
        sc_sb = [cut(G * H) for _ in range(HALVES)]
        th_sb = [cut(G * H) for _ in range(HALVES)]
        e_sb = [cut(G * H) for _ in range(HALVES)]
        xv_sb = [cut(G * XW).rearrange("p (r c) -> p r c", r=G) for _ in range(HALVES)]
        sx_sb = [cut(G * H * XW).rearrange("p (r h c) -> p r h c", r=G, h=H) for _ in range(HALVES)]
        idx_sb = [cut(G, I32) for _ in range(HALVES)]
        zeros = cut(HD)
        assert used[0] <= staged_at
        xi_sb = [cut(ROWI) for _ in range(2)]
        rec_sb = [cut(REC, I32) for _ in range(2)]
        num_sb = [cut(1, I32) for _ in range(2)]
        used[0] = 0
        aggn = cut(TS * HD).rearrange("p (k c) -> p k c", k=TS)
        aggnT = cut(H * SW).rearrange("p (h i) -> p h i", h=H)
        ylin = cut(H * SW).rearrange("p (h i) -> p h i", h=H)
        yleak = cut(H * SW).rearrange("p (h i) -> p h i", h=H)
        yC = cut(SW)
        oC = cut(SW)
        statC = cut(TS * 6).rearrange("p (k c) -> p k c", k=TS)
        mvC = cut(TS * 2).rearrange("p (k c) -> p k c", k=TS)
        rstdC = cut(TS)
        rzC = cut(TS * H)
        numC = sb("numC", [P, TS], I32)[:, :]
        eps = sb("eps", [P, 1])

        banks = [ps(f"bank{i}", [P, 512]) for i in range(8)]
        b_aggT, b_n, b_s, b_x, b_1, b_2, b_pq, b_ctl = banks
        agg_ps = [banks[0], banks[1]]
        z_ps = [banks[2], banks[3]]
        lin_ps = banks[0:4]
        bT_ps = banks[4:6]
        bO_ps = banks[6]

        s_w = sem("weights_in")
        s_xT = sem("xT_in")
        s_nat = [sem(f"nat_in{b}") for b in range(2)]
        s_adjT = [sem(f"adjT_in{q}") for q in range(PIECES)]
        s_ident = sem("ident_ready")
        s_const = sem("dve_consts")
        s_abc = sem("a_bc_ready")
        s_v = sem("v_products")
        s_vsb = sem("v_ready")
        s_natdve = sem("nat_searched")
        s_natact = sem("nat_counted")
        s_pass = sem("nat_passes")
        s_piece = sem("adjT_used")
        s_aggT = sem("aggT_copied")
        s_ns = sem("layer0_products")
        s_var = sem("var_ready")
        s_std = sem("std_ready")
        s_xp = sem("xp_ready")
        s_xpTps = sem("xpT_transposed")
        s_xpT = sem("xpT_copied")
        s_pq = sem("pq_products")
        s_12 = sem("x12_products")
        s_12c = sem("x12_copied")
        s_gmax = sem("worst_row")
        s_gone = sem("worst_of_all")
        s_gbc = sem("general_known")
        s_gT = sem("worst_transposed")
        s_hot = sem("onehots_ready")
        s_count = sem("lengths_counted")
        s_pos = sem("places_ready")
        s_stage = [sem(f"record_staged{b}") for b in range(2)]
        s_rec = [sem(f"record_placed{b}") for b in range(2)]
        s_recin = [sem(f"records_in{b}") for b in range(2)]
        s_num = [sem(f"numbers_copied{b}") for b in range(2)]
        s_numk = sem("tile_numbers_kept")
        s_kept = sem("tile_rows_kept")
        s_recms = sem("records_blank")
        s_numC = sem("out_numbers")
        s_fresh = sem("gathers_recounted")
        s_rx = sem("row_xp_copied")
        s_rows = [sem(f"rows_stored{b}") for b in range(2)]
        s_chain = sem("dve_chain")
        s_ctl = sem("ctl_ready")
        s_xi = [sem(f"xi_in{b}") for b in range(2)]
        s_blk = sem("block_in")
        s_pdve = sem("dve_waits_passed")
        s_ppool = sem("pool_waits_passed")
        s_psp = sem("sp_waits_passed")
        s_pact = sem("act_waits_passed")
        s_zero = sem("zeros_ready")
        s_idx = [sem(f"idx_copied{b}") for b in range(HALVES)]
        s_g = [sem(f"gathered{b}") for b in range(HALVES)]
        s_z = [sem(f"z_ready{b}") for b in range(HALVES)]
        s_acc = [sem(f"sums_ready{b}") for b in range(HALVES)]
        s_sc = [sem(f"scores_ready{b}") for b in range(HALVES)]
        s_th = [sem(f"tanh_ready{b}") for b in range(HALVES)]
        s_e = [sem(f"exp_ready{b}") for b in range(HALVES)]
        s_xv = [sem(f"xv_ready{b}") for b in range(HALVES)]
        s_sx = [sem(f"sx_ready{b}") for b in range(HALVES)]
        s_sum = [sem(f"sx_summed{b}") for b in range(HALVES)]
        s_tdve = sem("tile_scored")
        s_tpe = sem("tile_summed")
        s_evac = sem("tile_copied")
        s_rz = sem("rz_ready")
        s_aggn = sem("aggn_ready")
        s_aTps = sem("aggnT_transposed")
        s_aT = sem("aggnT_copied")
        s_lin = sem("lin_products")
        s_linc = sem("lin_copied")
        s_leak = sem("leaky_ready")
        s_o = sem("out_products")
        s_cC = sem("dve_chain_last")
        s_varC = sem("varC_ready")
        s_stdC = sem("stdC_ready")
        s_oC = sem("out_ready")
        s_out = sem("out_stored")

        CTL_A, CTL_B, CTL_A0, CTL_B0, CTL_GA, CTL_GB, CTL_NB, CTL_GEN = 0, T, 2 * T, 3 * T, 4 * T, 5 * T, 6 * T, 6 * T + 1

        def ctl_value(eng, at, low, high):
            return eng.value_load(ctl[0:1, bass.ds(at, 1)], min_val=low, max_val=high)

        MAXN = T * NBLK * TURNS

        def tile_counts(eng, t):
            return (ctl_value(eng, t + CTL_A, 1, TURNS), ctl_value(eng, t + CTL_B, 0, TURNS),
                    ctl_value(eng, t + CTL_A0, 0, MAXN), ctl_value(eng, t + CTL_B0, 0, MAXN))

        def gather_counts(eng, t):
            return ctl_value(eng, t + CTL_GA, 0, MAXN), ctl_value(eng, t + CTL_GB, 0, MAXN)

        def recounted(eng, passed, gen, t, blk):
            with eng.If(gen > 0):
                eng.wait_ge(s_fresh, t * NBLK + blk)
                apart(eng, passed)

        def apart(eng, passed):
            eng.sem_inc(passed, 1)

        block = ctx.enter_context(nc.Block())

        @block.sync
        def _(sp):
            sp.dma_start(h_sb, x.rearrange("(t p) d -> p t d", p=P)).then_inc(s_w, 16)
            sp.dma_start(lane_sb, lane.to_broadcast((P, CAND))).then_inc(s_w, 16)
            sp.dma_start(wself_sb[:, :], w_self).then_inc(s_w, 16)
            sp.dma_start(wneigh_sb[:, :], w_neigh).then_inc(s_w, 16)
            sp.dma_start(w1_sb[:, :, :], w1.rearrange("h c k -> c h k")).then_inc(s_w, 16)
            sp.dma_start(w2_sb[:, :, :], w2.rearrange("h c k -> c h k")).then_inc(s_w, 16)
            sp.dma_start(w12t[:, 0], w1_t.rearrange("h k c -> k h c")).then_inc(s_w, 16)
            sp.dma_start(w12t[:, 1], w2_t.rearrange("h k c -> k h c")).then_inc(s_w, 16)
            sp.dma_start(acol_sb, a_col).then_inc(s_w, 16)
            sp.dma_start(a_bc[:, :], a_row.to_broadcast((P, HD))).then_inc(s_w, 16)
            sp.dma_start(wlin_sb[:, :, :], wlin_t.rearrange("h d o -> d h o")).then_inc(s_w, 16)
            sp.dma_start(wout_sb[:, :, :], w_out.rearrange("(h o) n -> o h n", h=H)).then_inc(s_w, 16)
            sp.dma_start(bins_sb, bins.to_broadcast((P, BINS))).then_inc(s_w, 16)
            sp.dma_start(ends_sb, ends.to_broadcast((P, T))).then_inc(s_w, 16)
            with sp.Fori(0, STRIPS) as s:
                for k in range(TS):
                    sp.wait_ge(s_natdve, s * TS + (k + 1))
                    sp.wait_ge(s_natact, s * TS + (k + 1))
                    sp.dma_start(nat[k % 2], adj[bass.ds(s * SW + k * P, P), :]).then_inc(s_nat[k % 2], 16)
                    sp.wait_ge(s_piece, s * PIECES + (k + 1))
                    apart(sp, s_psp)
                    sp.dma_start(adjT_sb[:, k], adj_t[k * JT * P:(k + 1) * JT * P, bass.ds(s * SW, SW)]
                                 .rearrange("(j p) i -> p j i", p=P)).then_inc(s_adjT[k], 16)
                    if k == 1:
                        sp.wait_ge(s_ns, s)
                        sp.dma_start(xTs, x_t[:, bass.ds(s * SW, SW)]).then_inc(s_xT, 16)

            sp.wait_ge(s_ctl, 1)
            for b in range(2):
                sp.wait_ge(s_rec[b], 16 * T // 2)
            nblk = ctl_value(sp, CTL_NB, 1, NBLK)
            gen = ctl_value(sp, CTL_GEN, 0, 1)
            with sp.Fori(0, T // 2) as tt:
                for u in range(2):
                    sp.wait_ge(s_tpe, tt * 2 + (u + 1))
                    sp.dma_start(rec_sb[u], records[bass.ds(tt * (2 * P) + u * P, P), :]).then_inc(s_recin[u], 16)
                    with sp.If(gen > 0):
                        before_a = ctl_value(sp, tt * 2 + (u + CTL_A0), 0, MAXN)
                        before_b = ctl_value(sp, tt * 2 + (u + CTL_B0), 0, MAXN)
                        sp.wait_ge(s_recin[u], tt * 16 + 16)
                        apart(sp, s_psp)
                        with sp.Fori(0, nblk) as blk:
                            for b, before in ((0, before_a), (1, before_b)):
                                sp.wait_ge(s_xv[b], before + blk * TURNS)
                                apart(sp, s_psp)
                                sp.wait_ge(s_idx[b], before + blk * TURNS)
                                apart(sp, s_psp)
                            sp.dma_start(rec_sb[u][:, VAL:VAL + BLOCK].bitcast(F32),
                                         adj[bass.ds(tt * (2 * P) + u * P, P), bass.ds(blk * BLOCK, BLOCK)]
                                         ).then_inc(s_blk, 16)
                            sp.dma_start(rec_sb[u][:, IDX:IDX + BLOCK],
                                         columns[:, bass.ds(blk * BLOCK, BLOCK)].to_broadcast((P, BLOCK))
                                         ).then_inc(s_blk, 16)
                        sp.nop()
                    sp.nop()

        @block.gpsimd
        def _(pool):
            nc.gpsimd.memset(ident[:, :], 0.0).then_inc(s_ident, 1)
            pool.wait_ge(s_ident, 1)
            nc.gpsimd.affine_select(out=ident[:, :], in_=ident[:, :], compare_op=ALU.not_equal, fill=1.0, base=0,
                                    pattern=[[-1, P]], channel_multiplier=1).then_inc(s_ident, 1)
            nc.gpsimd.memset(ones_h[:, :], 1.0).then_inc(s_ident, 1)
            nc.gpsimd.memset(ones_f[:, :], 1.0).then_inc(s_ident, 1)
            pool.wait_ge(s_ident, 4)
            nc.gpsimd.affine_select(out=before_h[:, :], in_=ones_h[:, :], compare_op=ALU.is_gt, fill=0.0, base=0,
                                    pattern=[[1, P]], channel_multiplier=-1).then_inc(s_ident, 1)
            nc.gpsimd.memset(rec_all[:, :, :], 0).then_inc(s_recms, 1)
            pool.wait_ge(s_recms, 1)
            nc.gpsimd.iota(rec_all[:, :, NUM], pattern=[[P, T]], base=0, channel_multiplier=1).then_inc(s_recms, 1)
            with pool.Fori(0, STRIPS) as s:
                pool.wait_ge(s_xp, s + 1)
                for k in range(TS):
                    b = k % 2
                    pool.wait_ge(s_rows[b], s * (2 * 32) + (k // 2) * 32)
                    apart(pool, s_ppool)
                    nc.gpsimd.tensor_copy(row_j[b][:, ZW:ZW + D], xpA[:, k * D:(k + 1) * D]).then_inc(s_rx, 1)
                    nc.gpsimd.tensor_copy(row_i[b][:, ZW:ZW + D], xpA[:, k * D:(k + 1) * D]).then_inc(s_rx, 1)
                    pool.wait_ge(s_rx, s * (2 * TS) + (2 * k + 2))
                    pool.wait_ge(s_12c, s * TS + (k + 1))
                    pool.dma_start(table_j[bass.ds(s * SW + k * P, P), :], row_j[b]).then_inc(s_rows[b], 16)
                    pool.dma_start(table_i[bass.ds(s * SW + k * P, P), :], row_i[b]).then_inc(s_rows[b], 16)

            pool.wait_ge(s_pos, 1)
            with pool.Fori(0, T // 2) as tt:
                for b in range(2):
                    pool.wait_ge(s_rec[b], tt * 16)
                    apart(pool, s_ppool)
                    nc.gpsimd.tensor_copy(stage[b], rec_all[:, tt * 2 + b, :]).then_inc(s_stage[b], 1)
                    nc.gpsimd.tensor_copy(stage_pos[b], pos_all[:, bass.ds(tt * 2 + b, 1)]).then_inc(s_stage[b], 1)
                    pool.wait_ge(s_stage[b], tt * 2 + 2)
                    apart(pool, s_ppool)
                    nc.gpsimd.indirect_dma_start(records, bass.IndirectOffsetOnAxis(ap=stage_pos[b], axis=0),
                                                 stage[b], None).then_inc(s_rec[b], 16)

            for b in range(2):
                pool.wait_ge(s_rows[b], 2 * 16 * T // 2)
            pool.wait_ge(s_ctl, 1)
            nblk = ctl_value(pool, CTL_NB, 1, NBLK)
            gen = ctl_value(pool, CTL_GEN, 0, 1)

            def gather(b, n, u, slot):
                pool.wait_ge(s_z[b], n)
                pool.wait_ge(s_xv[b], n)
                apart(pool, s_ppool)
                nc.gpsimd.tensor_copy(idx_sb[b], rec_sb[u][:, bass.ds(slot + IDX, G)]).then_inc(s_idx[b], 1)
                pool.wait_ge(s_idx[b], n + 1)
                apart(pool, s_ppool)
                for r in range(G):
                    nc.gpsimd.indirect_dma_start(
                        g_sb[b][:, r, :], None, table_j,
                        bass.IndirectOffsetOnAxis(ap=idx_sb[b][:, r:r + 1], axis=0)).then_inc(s_g[b], 16)

            def gather_own(u, m):
                pool.wait_ge(s_recin[u], m * 16 + 16)
                pool.wait_ge(s_tdve, m * 2 + (u + 1))
                pool.wait_ge(s_kept, m * 2 + (u + 1))
                pool.wait_ge(s_numk, m * 2 + (u + 1))
                apart(pool, s_ppool)
                nc.gpsimd.tensor_copy(num_sb[u], rec_sb[u][:, NUM:NUM + 1]).then_inc(s_num[u], 1)
                pool.wait_ge(s_num[u], m + 1)
                apart(pool, s_ppool)
                nc.gpsimd.indirect_dma_start(xi_sb[u], None, table_i,
                                             bass.IndirectOffsetOnAxis(ap=num_sb[u], axis=0)).then_inc(s_xi[u], 16)

            pool.sem_inc(s_kept, 2)
            pool.sem_inc(s_numk, 2)
            gather_own(0, 0)
            with pool.Fori(0, T // 2) as tt:
                for u in range(2):
                    t = tt * 2 + u
                    turns_a, turns_b, before_a, before_b = tile_counts(pool, t)
                    with pool.Fori(0, nblk) as blk:
                        with pool.If(gen > 0):
                            pool.wait_ge(s_blk, tt * (2 * 32 * NBLK) + blk * 32 + (u * 32 * NBLK + 32))
                            pool.nop()
                        with pool.Fori(0, turns_a) as i:
                            gather(0, before_a + blk * TURNS + i, u, i * (2 * G))
                            with pool.If(i < turns_b):
                                gather(1, before_b + blk * TURNS + i, u, i * (2 * G) + G)
                                pool.nop()
                            pool.nop()
                        with pool.If(gen > 0):
                            for b, before in ((0, before_a), (1, before_b)):
                                pool.wait_ge(s_z[b], before + blk * TURNS + TURNS)
                                pool.wait_ge(s_xv[b], before + blk * TURNS + TURNS)
                            apart(pool, s_ppool)
                            pool.inc_swdge_sem(s_g, [16 * G * TURNS] * HALVES, mode="sub")
                            pool.sem_inc(s_fresh, 1)
                        pool.nop()
                    pool.wait_ge(s_xi[u], tt * 16 + 16)
                    apart(pool, s_ppool)
                    nc.gpsimd.tensor_copy(num_all[:, bass.ds(t, 1)], num_sb[u]).then_inc(s_numk, 1)
                    nc.gpsimd.tensor_copy(xs_all[:, t, :], xi_sb[u][:, ZW:ZW + D]).then_inc(s_kept, 1)
                    if u == 0:
                        gather_own(1, tt)
                    else:
                        with pool.If(tt < T // 2 - 1):
                            gather_own(0, tt + 1)
                            pool.nop()
                        pool.nop()

            with pool.Fori(0, STRIPS) as s:
                pool.wait_ge(s_out, s * (16 * TS))
                apart(pool, s_ppool)
                nc.gpsimd.tensor_copy(numC, num_all[:, bass.ds(s * TS, TS)]).then_inc(s_numC, 1)
                pool.wait_ge(s_numC, s + 1)
                pool.wait_ge(s_oC, s + 1)
                apart(pool, s_ppool)
                for k in range(TS):
                    nc.gpsimd.indirect_dma_start(out, bass.IndirectOffsetOnAxis(ap=numC[:, k:k + 1], axis=0),
                                                 oC[:, k * D:(k + 1) * D], None).then_inc(s_out, 16)
            pool.wait_ge(s_out, 16 * T)

        @block.vector
        def _(dve):
            v = nc.vector
            chain = [0, 0]

            def link(ins):
                ins.then_inc(s_chain, 1)
                chain[0] += 1

            def settle(alone=False):
                dve.wait_ge(s_chain, chain[1] * LINKS + chain[0])
                if alone:
                    apart(dve, s_pdve)

            dve.sem_inc(s_natdve, 2)
            dve.sem_inc(s_tdve, 2)
            dve.sem_inc(s_evac, 2)
            v.memset(eps[:, :], EPS).then_inc(s_const, 1)
            for b in range(2):
                v.memset(row_j[b][:, ROWJ - 1:ROWJ], 1.0).then_inc(s_const, 1)
            dve.wait_ge(s_w, 16 * LOADS)
            dve.wait_ge(s_recms, 2)
            v.tensor_scalar(a_bc[:, :], a_bc[:, :], POS, None, ALU.mult).then_inc(s_abc, 1)
            dve.wait_ge(s_v, 1)
            v.tensor_scalar(v1_sb[:, :], b_pq[:, 0:H], LIN, None, ALU.mult).then_inc(s_vsb, 1)
            v.tensor_scalar(v2_sb[:, :], b_pq[:, H:2 * H], LIN, None, ALU.mult).then_inc(s_vsb, 1)

            LINKS = 89
            with dve.Fori(0, STRIPS) as s:
                chain[:] = [0, s]
                for k in range(TS):
                    b = k % 2
                    dve.wait_ge(s_nat[b], s * 32 + 16 * (k // 2 + 1))
                    apart(dve, s_pdve)
                    for c in range(NCH):
                        last = v.max(cand[b][:, 8 * c:8 * c + 8], nat[b][:, c * CH:(c + 1) * CH])
                    link(last)
                    settle(alone=True)
                    for c in range(NCH):
                        last = v.max_index(cand_i[b][:, 8 * c:8 * c + 8], cand[b][:, 8 * c:8 * c + 8],
                                           nat[b][:, c * CH:(c + 1) * CH])
                    last.then_inc(s_natdve, 1)
                    link(v.scalar_tensor_tensor(keep, cand[b], 0.0, lane_sb, ALU.is_gt, ALU.mult))
                    link(v.tensor_scalar(part[0], cand[b].bitcast(I32), 16, None, ALU.logical_shift_right))
                    link(v.tensor_scalar(part[1], cand[b].bitcast(I32), 0xffff, None, ALU.bitwise_and))
                    dve.wait_ge(s_natdve, s * TS + (k + 3))
                    link(v.scalar_tensor_tensor(comp[b][2], cand[b], 0.0, cand_i[b], ALU.is_gt, ALU.mult))
                    settle()
                    link(v.tensor_tensor(comp[b][0], keep, part[0], ALU.add))
                    link(v.tensor_tensor(comp[b][1], keep, part[1], ALU.add))
                    link(v.tensor_tensor(comp[b][2], keep, comp[b][2], ALU.add))
                    settle(alone=True)
                    for r in range(ROUNDS):
                        for c in range(3):
                            last = v.max(best[:, c, k, 8 * r:8 * r + 8], comp[b][c])
                        link(last)
                        if r < ROUNDS - 1:
                            settle(alone=True)
                            for c in range(3):
                                last = v.match_replace(comp[b][c], best[:, c, k, 8 * r:8 * r + 8], comp[b][c], 0.0)
                            link(last)
                            settle(alone=True)
                settle()
                for c in range(3):
                    last = v.tensor_scalar(dec[:, c], best[:, c], 1.0, 0.0, ALU.subtract, ALU.max)
                link(last)
                settle()
                link(v.tensor_scalar(best[:, 0].bitcast(I32), dec[:, 0], 0xffff, 16, ALU.bitwise_and,
                                     ALU.logical_shift_left))
                link(v.tensor_scalar(best[:, 1].bitcast(I32), dec[:, 1], 0xffff, None, ALU.bitwise_and))
                link(v.tensor_scalar(best[:, 2].bitcast(I32), dec[:, 2], KEY + 3, 8, ALU.logical_shift_right,
                                     ALU.logical_shift_left))
                link(v.tensor_scalar(dec_i, dec[:, 2], CH - 1, None, ALU.bitwise_and))
                settle()
                at_val = rec_all[:, bass.ds(s * TS, TS), VAL:VAL + SLOTS]
                at_idx = rec_all[:, bass.ds(s * TS, TS), IDX:IDX + SLOTS]
                link(v.tensor_tensor(at_val, best[:, 0].bitcast(I32),
                                     best[:, 1].bitcast(I32), ALU.bitwise_or))
                link(v.tensor_tensor(at_idx, best[:, 2].bitcast(I32), dec_i,
                                     ALU.bitwise_or))
                settle()
                link(v.tensor_scalar(best[:, 0], at_val.bitcast(F32), 0.0, None, ALU.is_gt))
                settle()
                link(v.tensor_reduce(found[:, bass.ds(s * TS, TS)], best[:, 0], AX, ALU.add))

                dve.wait_ge(s_natact, s * TS + (TS + 2))
                link(v.tensor_scalar(rdeg, deg_all[:, bass.ds(s * TS, TS)], 1.0, None, ALU.max))
                settle()
                link(v.reciprocal(rdeg, rdeg))
                settle()
                dve.wait_ge(s_ns, s + 1)
                for k in range(TS):
                    link(v.scalar_tensor_tensor(yA[:, k * D:(k + 1) * D], b_n[:, k * D:(k + 1) * D],
                                                rdeg[:, k:k + 1], h_sb[:, s * TS + k, :], ALU.mult, ALU.add))
                settle()
                link(v.tensor_tensor(yA, yA, b_s[:, :], ALU.add))
                settle()
                for k in range(TS):
                    link(v.bn_stats(stat[:, k, :], yA[:, k * D:(k + 1) * D]))
                settle(alone=True)
                for k in range(TS):
                    last = v.bn_aggr(mv[:, k, :], stat[:, k, :])
                last.then_inc(s_var, 1)
                dve.wait_ge(s_std, s + 1)
                link(v.reciprocal(rstd, rstd))
                settle()
                dve.wait_ge(s_xpTps, s)
                dve.wait_ge(s_rx, s * (2 * TS))
                for k in range(TS):
                    last = v.tensor_scalar(xpA[:, k * D:(k + 1) * D], yA[:, k * D:(k + 1) * D], mv[:, k, 0:1],
                                           rstd[:, k:k + 1], ALU.subtract, ALU.mult)
                last.then_inc(s_xp, 1)
                assert chain[0] == LINKS, chain

            c = [0]

            def step(ins):
                ins.then_inc(s_cC, 1)
                c[0] += 1
                dve.wait_ge(s_cC, c[0])

            dve.wait_ge(s_chain, STRIPS * LINKS)
            step(v.tensor_tensor(bad, found, cnt_all, ALU.subtract))
            step(v.tensor_tensor(bad, bad, bad, ALU.mult))
            step(v.tensor_tensor(bad, bad, neg_all, ALU.add))
            v.tensor_reduce(gen_sb[:, 0:1], bad, AX, ALU.max).then_inc(s_gmax, 1)
            dve.wait_ge(s_gT, 1)
            v.tensor_reduce(gen_sb[0:1, 1:2], b_ctl[0:1, 0:P], AX, ALU.max).then_inc(s_gone, 1)
            dve.wait_ge(s_gbc, 1)
            gen = gen_sb[:, 2:3]
            step(v.tensor_scalar(gen, b_ctl[:, 256:257], 0.0, None, ALU.is_gt))
            R = [crow[:, i * T:(i + 1) * T] for i in range(8)]
            I = [irow[:, i * T:(i + 1) * T] for i in range(4)]
            few = gen_sb[:, 3:4]
            step(v.tensor_scalar(few, gen, -1.0, 1.0, ALU.mult, ALU.add))
            step(v.tensor_scalar(R[0], cnt_all, few, float(BINS - 1), ALU.mult, ALU.min))
            v.tensor_tensor(onehot, R[0].rearrange("p (t o) -> p t o", o=1).to_broadcast((P, T, BINS)),
                            bins_sb.rearrange("p (o b) -> p o b", o=1).to_broadcast((P, T, BINS)),
                            ALU.is_equal).then_inc(s_hot, 1)
            dve.wait_ge(s_count, 1)
            C = 512 // BINS
            for i in range(T // C):
                last = v.tensor_copy(total[:, :, i * C:(i + 1) * C].rearrange("p b t -> p t b"),
                                     banks[i][:, :].rearrange("p (t b) -> p t b", t=C))
            step(last)
            flat = nat[0][:, 0:NB_]
            step(v.tensor_tensor_scan(nat[0][:, NB_:2 * NB_], ones_f[:, 0:1].to_broadcast((P, NB_)), flat, 0.0,
                                      ALU.mult, ALU.add))
            step(v.tensor_tensor(flat, nat[0][:, NB_:2 * NB_], flat, ALU.subtract))
            for i in range(T // C):
                last = v.tensor_tensor(place[:, i * C:(i + 1) * C, :],
                                       total[:, :, i * C:(i + 1) * C].rearrange("p b t -> p t b"),
                                       banks[4 + i][:, :].rearrange("p (t b) -> p t b", t=C), ALU.add)
            step(last)
            step(v.tensor_tensor(place, place, onehot, ALU.mult))
            step(v.tensor_reduce(R[1], place, AX, ALU.add))
            v.tensor_copy(pos_all[:, :], R[1]).then_inc(s_pos, 1)
            step(v.tensor_tensor(place, upto[:, :, T - 1:T].rearrange("p b o -> p o b").to_broadcast((P, T, BINS)),
                                 ends_sb.rearrange("p (t o) -> p t o", o=1).to_broadcast((P, T, BINS)), ALU.is_lt))
            step(v.tensor_reduce(R[0], place, AX, ALU.add))
            R = [r[0:1, :] for r in R]
            I = [i[0:1, :] for i in I]
            gen, few = gen[0:1, :], few[0:1, :]
            step(v.tensor_scalar(I[0], R[0], float(G - 1), None, ALU.add))
            step(v.tensor_scalar(I[0], I[0], 2, None, ALU.logical_shift_right))
            step(v.tensor_copy(R[3], I[0]))
            step(v.tensor_scalar(R[3], R[3], 1.0, None, ALU.max))
            step(v.tensor_scalar(R[4], R[3], -1.0, float(BLOCK // G), ALU.mult, ALU.add))
            step(v.scalar_tensor_tensor(R[3], R[4], gen, R[3], ALU.mult, ALU.add))
            step(v.tensor_copy(I[1], R[3]))
            step(v.tensor_scalar(I[0], R[3], 1.0, None, ALU.add))
            step(v.tensor_scalar(ctl[0:1, CTL_A:CTL_A + T], I[0], 1, None, ALU.logical_shift_right))
            step(v.tensor_scalar(ctl[0:1, CTL_B:CTL_B + T], I[1], 1, None, ALU.logical_shift_right))
            step(v.tensor_scalar(R[2][:, 1:2], gen, float(NBLK - 1), 1.0, ALU.mult, ALU.add))
            step(v.tensor_copy(ctl[0:1, CTL_GEN:CTL_GEN + 1], gen))
            step(v.tensor_copy(ctl[0:1, CTL_NB:CTL_NB + 1], R[2][:, 1:2]))
            step(v.memset(R[7], 1.0))
            for at, to, to_g in ((CTL_A, CTL_A0, CTL_GA), (CTL_B, CTL_B0, CTL_GB)):
                step(v.tensor_scalar(R[4], ctl[0:1, at:at + T], R[2][:, 1:2], None, ALU.mult))
                step(v.tensor_tensor_scan(R[5], R[7], R[4], 0.0, ALU.mult, ALU.add))
                step(v.tensor_tensor(ctl[0:1, to:to + T], R[5], R[4], ALU.subtract))
                last = v.tensor_scalar(ctl[0:1, to_g:to_g + T], ctl[0:1, to:to + T], few, None, ALU.mult)
                if to == CTL_A0:
                    step(last)
            last.then_inc(s_ctl, 1)
            dve.wait_ge(s_ctl, 1)

            for b in range(2):
                dve.wait_ge(s_rows[b], 2 * 16 * T // 2)
            v.memset(zeros, 0.0).then_inc(s_zero, 1)
            nblk = ctl_value(dve, CTL_NB, 1, NBLK)
            gen = ctl_value(dve, CTL_GEN, 0, 1)

            def score(b, n, ng, u):
                dve.wait_ge(s_g[b], ng * (16 * G) + 16 * G)
                v.tensor_tensor(z_sb[b], g_sb[b][:, :, 0:ZW], xi_sb[u][:, 0:ZW].rearrange("p (o c) -> p o c", o=1)
                                .to_broadcast((P, G, ZW)), ALU.add).then_inc(s_z[b], 1)
                dve.wait_ge(s_z[b], n + 1)
                dve.wait_ge(s_th[b], n)
                for r in range(G):
                    for h in range(H):
                        last = v.scalar_tensor_tensor(z_sb[b][:, r, h * D:(h + 1) * D],
                                                      z_sb[b][:, r, h * D:(h + 1) * D], 0.0,
                                                      a_bc[:, h * D:(h + 1) * D], ALU.max, ALU.mult,
                                                      accum_out=sc_sb[b][:, r * H + h:r * H + h + 1])
                last.then_inc(s_acc[b], 1)
                dve.wait_ge(s_acc[b], n + 1)
                sc = sc_sb[b].rearrange("p (r h) -> p r h", r=G)
                v.tensor_tensor(sc, sc, z_sb[b][:, :, HD:ZW], ALU.add).then_inc(s_sc[b], 1)

            def evacuate(t, u):
                dve.wait_ge(s_tpe, t + 3)
                v.tensor_copy(agg_all[:, t, :], agg_ps[u][:, :])
                v.tensor_copy(z_all[:, t, :], z_ps[u][:, 0:H]).then_inc(s_evac, 1)

            def score_tile(t, u, xi_count):
                turns_a, turns_b, before_a, before_b = tile_counts(dve, t)
                from_a, from_b = gather_counts(dve, t)
                dve.wait_ge(s_xi[u], xi_count)
                apart(dve, s_pdve)
                with dve.Fori(0, nblk) as blk:
                    recounted(dve, s_pdve, gen, t, blk)
                    with dve.Fori(0, turns_a) as i:
                        score(0, before_a + blk * TURNS + i, from_a + i, u)
                        with dve.If(i < turns_b):
                            score(1, before_b + blk * TURNS + i, from_b + i, u)
                            dve.nop()
                        dve.nop()
                dve.drain().then_inc(s_tdve, 1)

            score_tile(0, 0, 16)
            with dve.Fori(0, T // 2 - 1) as tt:
                for u in (1, 0):
                    score_tile(tt * 2 + (2 - u), u, tt * 16 + (16 if u else 32))
                    evacuate(tt * 2 + (1 - u), 1 - u)
            score_tile(T - 1, 1, T // 2 * 16)
            evacuate(T - 2, 0)
            evacuate(T - 1, 1)

            dve.wait_ge(s_evac, T + 2)
            dve.wait_ge(s_kept, T + 2)
            LC = 4
            c0 = c[0]
            with dve.Fori(0, STRIPS) as s:
                n = [0]

                def step(ins):
                    ins.then_inc(s_cC, 1)
                    n[0] += 1
                    dve.wait_ge(s_cC, s * LC + (c0 + n[0]))

                step(v.reciprocal(rzC, z_all[:, bass.ds(s * TS, TS), :]))
                dve.wait_ge(s_aTps, s * H)
                for k in range(TS):
                    for h in range(H):
                        last = v.tensor_scalar(aggn[:, k, h * D:(h + 1) * D],
                                               agg_all[:, s * TS + k, h * D:(h + 1) * D],
                                               rzC[:, k * H + h:k * H + h + 1], None, ALU.mult)
                last.then_inc(s_aggn, 1)
                for h in range(H):
                    dve.wait_ge(s_linc, s * H + (h + 1))
                    if h == 0:
                        dve.wait_ge(s_o, s)
                    v.scalar_tensor_tensor(yleak[:, h, :], lin_ps[h][:, :], SLOPE, ylin[:, h, :], ALU.mult,
                                           ALU.max).then_inc(s_leak, 1)
                dve.wait_ge(s_o, s + 1)
                step(v.tensor_tensor(yC, bO_ps[:, :], xs_all[:, bass.ds(s * TS, TS), :].rearrange("p k d -> p (k d)"),
                                     ALU.add))
                for k in range(TS):
                    last = v.bn_stats(statC[:, k, :], yC[:, k * D:(k + 1) * D])
                step(last)
                apart(dve, s_pdve)
                for k in range(TS):
                    last = v.bn_aggr(mvC[:, k, :], statC[:, k, :])
                last.then_inc(s_varC, 1)
                dve.wait_ge(s_stdC, s + 1)
                step(v.reciprocal(rstdC, rstdC))
                dve.wait_ge(s_out, s * (16 * TS))
                for k in range(TS):
                    last = v.tensor_scalar(oC[:, k * D:(k + 1) * D], yC[:, k * D:(k + 1) * D], mvC[:, k, 0:1],
                                           rstdC[:, k:k + 1], ALU.subtract, ALU.mult)
                last.then_inc(s_oC, 1)
                assert n[0] == LC, n

        @block.scalar
        def _(act):
            a = nc.scalar
            act.sem_inc(s_natact, 2)
            act.wait_ge(s_const, 3)
            with act.Fori(0, STRIPS) as s:
                for k in range(TS):
                    b = k % 2
                    act.wait_ge(s_nat[b], s * 32 + 16 * (k // 2 + 1))
                    act.wait_ge(s_natact, s * TS + (k + 2))
                    a.activation(junk, nat[b], ACT.Copy,
                                 accum_out=deg_all[:, bass.ds(s * TS + k, 1)]).then_inc(s_pass, 1)
                    act.wait_ge(s_pass, s * (2 * TS) + (2 * k + 1))
                    a.activation(junk, nat[b], ACT.Sign,
                                 accum_out=cnt_all[:, bass.ds(s * TS + k, 1)]).then_inc(s_pass, 1)
                    act.wait_ge(s_pass, s * (2 * TS) + (2 * k + 2))
                    a.activation(junk, nat[b], ACT.Relu, scale=-1.0,
                                 accum_out=neg_all[:, bass.ds(s * TS + k, 1)]).then_inc(s_natact, 1)
                act.wait_ge(s_piece, s * PIECES + 2 * PIECES)
                act.wait_ge(s_ns, s)
                a.activation(aggT, b_aggT[:, :], ACT.Copy).then_inc(s_aggT, 1)
                act.wait_ge(s_var, s + 1)
                a.activation(rstd, mv[:, :, 1:2], ACT.Sqrt, bias=eps[:, 0:1]).then_inc(s_std, 1)
                act.wait_ge(s_xpTps, s + 1)
                act.wait_ge(s_12, s * TS)
                a.activation(xpT, b_x[:, :], ACT.Copy).then_inc(s_xpT, 1)
                for k in range(TS):
                    b = k % 2
                    act.wait_ge(s_12, s * TS + (k + 1))
                    act.wait_ge(s_rows[b], s * (2 * 32) + (k // 2) * 32)
                    a.activation(row_j[b][:, 0:HD], b_2[:, :], ACT.Copy)
                    a.activation(row_j[b][:, HD:ZW], b_pq[:, H:2 * H], ACT.Copy)
                    a.activation(row_i[b][:, HD:ZW], b_pq[:, 0:H], ACT.Copy)
                    a.activation(row_i[b][:, 0:HD], b_1[:, :], ACT.Copy).then_inc(s_12c, 1)

            act.wait_ge(s_ctl, 1)
            nblk = ctl_value(act, CTL_NB, 1, NBLK)

            gen = ctl_value(act, CTL_GEN, 0, 1)
            a.preload_act_table(ACT.Exp)

            def weigh(b, n, ng, u, slot):
                act.wait_ge(s_g[b], ng * (16 * G) + 16 * G)
                act.wait_ge(s_sx[b], n)
                for r in range(G):
                    last = a.activation(xv_sb[b][:, r, :], g_sb[b][:, r, ZW:ROWJ], ACT.Copy,
                                        scale=rec_sb[u][:, bass.ds(slot + (VAL + r), 1)].bitcast(F32))
                last.then_inc(s_xv[b], 1)
                act.wait_ge(s_sc[b], n + 1)
                a.activation(th_sb[b], sc_sb[b], ACT.Tanh, scale=0.125).then_inc(s_th[b], 1)
                act.wait_ge(s_th[b], n + 1)
                a.activation(e_sb[b], th_sb[b], ACT.Exp, scale=8.0).then_inc(s_e[b], 1)
                act.wait_ge(s_e[b], n + 1)
                act.wait_ge(s_xv[b], n + 1)
                act.wait_ge(s_sum[b], n)
                for r in range(G):
                    for h in range(H):
                        last = a.activation(sx_sb[b][:, r, h, :], xv_sb[b][:, r, :], ACT.Copy,
                                            scale=e_sb[b][:, r * H + h:r * H + h + 1])
                last.then_inc(s_sx[b], 1)

            with act.Fori(0, T // 2) as tt:
                for u in range(2):
                    t = tt * 2 + u
                    turns_a, turns_b, before_a, before_b = tile_counts(act, t)
                    from_a, from_b = gather_counts(act, t)
                    with act.Fori(0, nblk) as blk:
                        recounted(act, s_pact, gen, t, blk)
                        with act.Fori(0, turns_a) as i:
                            weigh(0, before_a + blk * TURNS + i, from_a + i, u, i * (2 * G))
                            with act.If(i < turns_b):
                                weigh(1, before_b + blk * TURNS + i, from_b + i, u, i * (2 * G) + G)
                                act.nop()
                            act.nop()

            with act.Fori(0, STRIPS) as s:
                for h in range(H):
                    act.wait_ge(s_aTps, s * H + (h + 1))
                    if h == 0:
                        act.wait_ge(s_lin, s * H)
                    a.activation(aggnT[:, h, :], bT_ps[h % 2][:, :], ACT.Copy).then_inc(s_aT, 1)
                for h in range(H):
                    act.wait_ge(s_lin, s * H + (h + 1))
                    if h == 0:
                        act.wait_ge(s_leak, s * H)
                    a.activation(ylin[:, h, :], lin_ps[h][:, :], ACT.Copy).then_inc(s_linc, 1)
                act.wait_ge(s_varC, s + 1)
                a.activation(rstdC, mvC[:, :, 1:2], ACT.Sqrt, bias=eps[:, 0:1]).then_inc(s_stdC, 1)

        @block.tensor
        def _(pe):
            mm = nc.tensor.matmul
            pe.sem_inc(s_piece, PIECES)
            pe.sem_inc(s_tpe, 2)
            pe.wait_ge(s_w, 16 * LOADS)
            for w in range(2):
                for h in range(H):
                    last = mm(b_pq[:, w * H + h:w * H + h + 1], w12t[:, w, h, :], acol_sb[:, h:h + 1],
                              start=True, stop=True)
            last.then_inc(s_v, 1)
            pe.wait_ge(s_ident, 5)
            pe.wait_ge(s_vsb, 2)
            with pe.Fori(0, STRIPS) as s:
                pe.wait_ge(s_aggT, s)
                for q in range(PIECES):
                    pe.wait_ge(s_adjT[q], s * 16 + 16)
                    for j in range(JT):
                        jt = q * JT + j
                        last = mm(b_aggT[:, :], h_sb[:, jt, :], adjT_sb[:, q, j, :], start=jt == 0, stop=jt == T - 1)
                    last.then_inc(s_piece, 1)
                pe.wait_ge(s_aggT, s + 1)
                pe.wait_ge(s_xT, s * 16 + 16)
                for k in range(TS):
                    mm(b_n[:, k * D:(k + 1) * D], aggT[:, k * P:(k + 1) * P], wneigh_sb[:, :], start=True, stop=True)
                    last = mm(b_s[:, k * D:(k + 1) * D], xTs[:, k * P:(k + 1) * P], wself_sb[:, :], start=True,
                              stop=True)
                last.then_inc(s_ns, 1)
                pe.wait_ge(s_xp, s + 1)
                pe.wait_ge(s_xpT, s)
                for k in range(TS):
                    last = nc.tensor.transpose(b_x[:, k * P:(k + 1) * P], xpA[:, k * D:(k + 1) * D], ident[:, :])
                last.then_inc(s_xpTps, 1)
                pe.wait_ge(s_xpT, s + 1)
                for k in range(TS):
                    pe.wait_ge(s_12c, s * TS + k)
                    xk = xpT[:, k * P:(k + 1) * P]
                    mm(b_1[:, :], xk, w1_sb[:, :, :].rearrange("p h k -> p (h k)"), start=True, stop=True)
                    mm(b_2[:, :], xk, w2_sb[:, :, :].rearrange("p h k -> p (h k)"), start=True, stop=True)
                    mm(b_pq[:, 0:H], xk, v1_sb[:, :], start=True, stop=True)
                    mm(b_pq[:, H:2 * H], xk, v2_sb[:, :], start=True, stop=True).then_inc(s_12, 1)

            pe.wait_ge(s_gmax, 1)
            mm(b_ctl[0:1, 0:P], gen_sb[:, 0:1], ident[:, :], start=True, stop=True).then_inc(s_gT, 1)
            pe.wait_ge(s_gone, 1)
            mm(b_ctl[:, 256:257], ones_f[0:1, :], gen_sb[0:1, 1:2], start=True, stop=True).then_inc(s_gbc, 1)
            pe.wait_ge(s_hot, 1)
            pe.wait_ge(s_12c, T)
            for i in range(T * BINS // 512):
                hot = onehot[:, i * (512 // BINS):(i + 1) * (512 // BINS), :].rearrange("p t b -> p (t b)")
                mm(banks[i][:, :], ones_h[:, :], hot, start=True, stop=True)
                last = mm(banks[4 + i][:, :], before_h[:, :], hot, start=True, stop=True)
            last.then_inc(s_count, 1)
            pe.wait_ge(s_ctl, 1)
            pe.wait_ge(s_12c, T)
            pe.wait_ge(s_zero, 1)
            nblk = ctl_value(pe, CTL_NB, 1, NBLK)

            def add_up(b, n, u):
                pe.wait_ge(s_sx[b], n + 1)
                for r in range(G):
                    mm(agg_ps[u][:, :], ident[:, :], sx_sb[b][:, r, :, 0:D], start=False, stop=False)
                    last = mm(z_ps[u][:, 0:H], ident[:, :], sx_sb[b][:, r, :, D:XW], start=False, stop=False)
                last.then_inc(s_sum[b], 1)

            with pe.Fori(0, T // 2) as tt:
                for u in range(2):
                    turns_a, turns_b, before_a, before_b = tile_counts(pe, tt * 2 + u)
                    pe.wait_ge(s_evac, tt * 2 + (u + 1))
                    mm(agg_ps[u][:, :], ident[:, :], zeros, start=True, stop=False)
                    mm(z_ps[u][:, 0:H], ident[:, :], zeros[:, 0:H], start=True, stop=False)
                    with pe.Fori(0, nblk) as blk:
                        with pe.Fori(0, turns_a) as i:
                            add_up(0, before_a + blk * TURNS + i, u)
                            with pe.If(i < turns_b):
                                add_up(1, before_b + blk * TURNS + i, u)
                                pe.nop()
                            pe.nop()
                    mm(agg_ps[u][:, :], ident[:, :], zeros, start=False, stop=True)
                    mm(z_ps[u][:, 0:H], ident[:, :], zeros[:, 0:H], start=False, stop=True).then_inc(s_tpe, 1)

            with pe.Fori(0, STRIPS) as s:
                pe.wait_ge(s_aggn, s + 1)
                for h in range(H):
                    pe.wait_ge(s_aT, s * H + max(h - 1, 0))
                    for k in range(TS):
                        last = nc.tensor.transpose(bT_ps[h % 2][:, k * P:(k + 1) * P],
                                                   aggn[:, k, h * D:(h + 1) * D], ident[:, :])
                    last.then_inc(s_aTps, 1)
                pe.wait_ge(s_leak, s * H)
                for h in range(H):
                    pe.wait_ge(s_aT, s * H + (h + 1))
                    mm(lin_ps[h][:, :], wlin_sb[:, h, :], aggnT[:, h, :], start=True, stop=True).then_inc(s_lin, 1)
                pe.wait_ge(s_leak, s * H + H)
                for k in range(TS):
                    for h in range(H):
                        last = mm(bO_ps[:, k * D:(k + 1) * D], yleak[:, h, k * P:(k + 1) * P], wout_sb[:, h, :],
                                  start=h == 0, stop=h == H - 1)
                last.then_inc(s_o, 1)


def kernel(x, adj, L0_gnn_W_self, L0_gnn_W_neigh, L1_gnn_w1, L1_gnn_w2, L1_gnn_a, L1_gnn_Wlin, L1_gnn_w):
    import numpy as np
    import concourse.bacc as bacc
    from concourse import mybir as mb
    from concourse.bass_utils import run_bass_kernel_spmd

    x, adj, a = np.asarray(x), np.asarray(adj), np.asarray(L1_gnn_a)
    w1, w2, wlin = np.asarray(L1_gnn_w1), np.asarray(L1_gnn_w2), np.asarray(L1_gnn_Wlin)
    n, d = x.shape
    candidates = n // 256 * 8
    arrays = {
        "x": x, "x_t": x.T, "adj": adj, "adj_t": adj.T,
        "w_self": np.asarray(L0_gnn_W_self), "w_neigh": np.asarray(L0_gnn_W_neigh),
        "w1": w1, "w2": w2, "w1_t": w1.transpose(0, 2, 1), "w2_t": w2.transpose(0, 2, 1),
        "a_row": a.reshape(1, -1), "a_col": a.T, "wlin_t": wlin.transpose(0, 2, 1), "w_out": np.asarray(L1_gnn_w),
        "lane": (np.arange(candidates) * 2.0 ** 17 + 1).astype(np.float32)[None, :],
        "columns": np.arange(n, dtype=np.int32)[None, :],
        "bins": np.arange(64, dtype=np.float32)[None, :],
        "ends": (np.arange(1, n // 128 + 1) * 128).astype(np.float32)[None, :],
    }
    arrays = {k: np.ascontiguousarray(v) for k, v in arrays.items()}
    nc = bacc.Bacc("TRN2", target_bir_lowering=False, num_devices=1)
    args = {k: nc.dram_tensor(k, v.shape, mb.dt.from_np(v.dtype), kind="ExternalInput").ap()
            for k, v in arrays.items()}
    out = nc.dram_tensor("out", (n, d), mb.dt.float32, kind="ExternalOutput").ap()
    two_layer_graph_kernel(nc, **args, out=out)
    r = run_bass_kernel_spmd(nc, [arrays], core_ids=[0])
    return r.results[0]["out"]
```
